# Optimizing a Trainium2 kernel written in Bass

```python
import numpy as np
import jax
import jax.numpy as jnp

def _softmax(x, axis=-1):
    return jax.nn.softmax(x, axis=axis)

def _gelu(x):
    return jax.nn.gelu(x, approximate=True)

def _silu(x):
    return jax.nn.silu(x)

def _sigmoid(x):
    return jax.nn.sigmoid(x)

def _layernorm(x, axis=-1, eps=1e-05):
    m = jnp.mean(x, axis=axis, keepdims=True)
    v = jnp.var(x, axis=axis, keepdims=True)
    return (x - m) / jnp.sqrt(v + eps)

def _scatter_add(tgt, idx, src, axis=0):
    return tgt.at[idx].add(src)

def _segment_sum(src, seg, n):
    return jax.ops.segment_sum(src, seg, n)
kernel_name = 'mk_rec_standalone_d1_rec_r8_aa93ec'

def setup_inputs(seed: int=0):
    np.random.seed(seed)
    _w = jnp.asarray

    def _rec_inputs():
        import jax
        import jax.numpy as jnp
        _rk = jax.random.key(seed)
        r_dense = -0.000171701 + 0.999137 * jax.random.normal(jax.random.fold_in(_rk, 1), (2048, 13), jnp.float32)
        r_sparse = jnp.stack([jax.random.randint(jax.random.fold_in(jax.random.fold_in(_rk, 2), 0), (2048,), 0, 9998, jnp.int32), jax.random.randint(jax.random.fold_in(jax.random.fold_in(_rk, 2), 1), (2048,), 2, 1250, jnp.int32), jax.random.randint(jax.random.fold_in(jax.random.fold_in(_rk, 2), 2), (2048,), 9, 9998, jnp.int32), jax.random.randint(jax.random.fold_in(jax.random.fold_in(_rk, 2), 3), (2048,), 2, 9995, jnp.int32), jax.random.randint(jax.random.fold_in(jax.random.fold_in(_rk, 2), 4), (2048,), 1, 9995, jnp.int32), jax.random.randint(jax.random.fold_in(jax.random.fold_in(_rk, 2), 5), (2048,), 1, 1250, jnp.int32), jax.random.randint(jax.random.fold_in(jax.random.fold_in(_rk, 2), 6), (2048,), 0, 9999, jnp.int32), jax.random.randint(jax.random.fold_in(jax.random.fold_in(_rk, 2), 7), (2048,), 0, 1250, jnp.int32), jax.random.randint(jax.random.fold_in(jax.random.fold_in(_rk, 2), 8), (2048,), 5, 9997, jnp.int32), jax.random.randint(jax.random.fold_in(jax.random.fold_in(_rk, 2), 9), (2048,), 1, 9999, jnp.int32), jax.random.randint(jax.random.fold_in(jax.random.fold_in(_rk, 2), 10), (2048,), 1, 9995, jnp.int32), jax.random.randint(jax.random.fold_in(jax.random.fold_in(_rk, 2), 11), (2048,), 2, 9997, jnp.int32), jax.random.randint(jax.random.fold_in(jax.random.fold_in(_rk, 2), 12), (2048,), 1, 9999, jnp.int32), jax.random.randint(jax.random.fold_in(jax.random.fold_in(_rk, 2), 13), (2048,), 2, 9995, jnp.int32), jax.random.randint(jax.random.fold_in(jax.random.fold_in(_rk, 2), 14), (2048,), 6, 1250, jnp.int32), jax.random.randint(jax.random.fold_in(jax.random.fold_in(_rk, 2), 15), (2048,), 0, 1250, jnp.int32), jax.random.randint(jax.random.fold_in(jax.random.fold_in(_rk, 2), 16), (2048,), 1, 9997, jnp.int32), jax.random.randint(jax.random.fold_in(jax.random.fold_in(_rk, 2), 17), (2048,), 2, 9996, jnp.int32), jax.random.randint(jax.random.fold_in(jax.random.fold_in(_rk, 2), 18), (2048,), 4, 1250, jnp.int32), jax.random.randint(jax.random.fold_in(jax.random.fold_in(_rk, 2), 19), (2048,), 3, 9993, jnp.int32), jax.random.randint(jax.random.fold_in(jax.random.fold_in(_rk, 2), 20), (2048,), 2, 9993, jnp.int32), jax.random.randint(jax.random.fold_in(jax.random.fold_in(_rk, 2), 21), (2048,), 2, 1250, jnp.int32), jax.random.randint(jax.random.fold_in(jax.random.fold_in(_rk, 2), 22), (2048,), 6, 1250, jnp.int32), jax.random.randint(jax.random.fold_in(jax.random.fold_in(_rk, 2), 23), (2048,), 0, 9999, jnp.int32), jax.random.randint(jax.random.fold_in(jax.random.fold_in(_rk, 2), 24), (2048,), 4, 9999, jnp.int32), jax.random.randint(jax.random.fold_in(jax.random.fold_in(_rk, 2), 25), (2048,), 0, 9999, jnp.int32)], axis=1)
        return (r_dense, r_sparse)
    r_dense, r_sparse = _rec_inputs()

    def _L0_rec_setup():
        import jax, jax.numpy as jnp
        import numpy as np
        B, M, V, E, ND = (512, 26, 1250, 32, 13)
        CIN_LAYERS = (128, 128)
        DEEP = (1024, 512, 256)
        DEEP_IN = M * E + ND
        CIN_CORES = sum((h - h // 2 for h in CIN_LAYERS))

        def _xdeepfm(sparse, dense, tables, lin_sparse_w, lin_dense_w, conv1_w, conv1_b, conv2_w, conv2_b, cin_w, cin_b, W1, b1, W2, b2, W3, b3, deep_w, deep_b, bias):
            feat_idx = jnp.arange(M)
            emb = tables[feat_idx, sparse]
            linear_out = lin_sparse_w[feat_idx, sparse].sum(-1) + dense @ lin_dense_w
            x0 = emb
            xk = emb
            res = []
            for w, bb in ((conv1_w, conv1_b), (conv2_w, conv2_b)):
                h = xk.shape[1]
                hp = jnp.einsum('bhd,bmd->bhmd', xk, x0).reshape(-1, h * M, E)
                xn = jax.nn.sigmoid(jnp.einsum('oi,bid->bod', w, hp) + bb[None, :, None])
                half = xn.shape[1] // 2
                xk = xn[:, :half]
                res.append(xn[:, half:])
            cin_feat = jnp.concatenate(res, axis=1).sum(-1)
            cin_out = (cin_feat @ cin_w + cin_b)[:, 0]
            deep_x = jnp.concatenate([emb.reshape(-1, M * E), dense], axis=-1)
            h1 = jnp.tanh(deep_x @ W1 + b1)
            h2 = jnp.tanh(h1 @ W2 + b2)
            h3 = jnp.tanh(h2 @ W3 + b3)
            deep_out = (h3 @ deep_w + deep_b)[:, 0]
            return linear_out + cin_out + deep_out + bias[0]
        key = jax.random.key(seed)
        ks = jax.random.split(key, 20)

        def n(k, shp, s=0.05):
            return jax.random.normal(k, shp, dtype=jnp.float32) * s
        inp = {}
        inp['sparse'] = jax.random.randint(ks[0], (B, M), 0, V)
        inp['dense'] = jax.random.normal(ks[1], (B, ND), dtype=jnp.float32)
        inp['tables'] = n(ks[2], (M, V, E))
        inp['lin_sparse_w'] = n(ks[3], (M, V))
        inp['lin_dense_w'] = n(ks[4], (ND,))
        inp['conv1_w'] = n(ks[5], (CIN_LAYERS[0], M * M))
        inp['conv1_b'] = jnp.zeros((CIN_LAYERS[0],), jnp.float32)
        inp['conv2_w'] = n(ks[6], (CIN_LAYERS[1], CIN_LAYERS[0] // 2 * M))
        inp['conv2_b'] = jnp.zeros((CIN_LAYERS[1],), jnp.float32)
        inp['cin_w'] = n(ks[7], (CIN_CORES, 1))
        inp['cin_b'] = jnp.zeros((1,), jnp.float32)
        dims = [DEEP_IN] + list(DEEP)
        inp['W1'] = n(ks[8], (dims[0], dims[1]))
        inp['b1'] = jnp.zeros((dims[1],), jnp.float32)
        inp['W2'] = n(ks[9], (dims[1], dims[2]))
        inp['b2'] = jnp.zeros((dims[2],), jnp.float32)
        inp['W3'] = n(ks[10], (dims[2], dims[3]))
        inp['b3'] = jnp.zeros((dims[3],), jnp.float32)
        inp['deep_w'] = n(ks[11], (dims[3], 1))
        inp['deep_b'] = jnp.zeros((1,), jnp.float32)
        inp['bias'] = jnp.zeros((1,), jnp.float32)
        return inp
    _L0_rec_all = _L0_rec_setup()
    _L0_rec_in = {k: v for k, v in _L0_rec_all.items() if k in ('tables', 'lin_sparse_w', 'lin_dense_w', 'conv1_w', 'conv1_b', 'conv2_w', 'conv2_b', 'cin_w', 'cin_b', 'W1', 'b1', 'W2', 'b2', 'W3', 'b3', 'deep_w', 'deep_b', 'bias')}
    del _L0_rec_all
    return {'r_dense': r_dense, 'r_sparse': r_sparse, 'L0_rec_tables': _L0_rec_in['tables'], 'L0_rec_lin_sparse_w': _L0_rec_in['lin_sparse_w'], 'L0_rec_lin_dense_w': _L0_rec_in['lin_dense_w'], 'L0_rec_conv1_w': _L0_rec_in['conv1_w'], 'L0_rec_conv1_b': _L0_rec_in['conv1_b'], 'L0_rec_conv2_w': _L0_rec_in['conv2_w'], 'L0_rec_conv2_b': _L0_rec_in['conv2_b'], 'L0_rec_cin_w': _L0_rec_in['cin_w'], 'L0_rec_cin_b': _L0_rec_in['cin_b'], 'L0_rec_W1': _L0_rec_in['W1'], 'L0_rec_b1': _L0_rec_in['b1'], 'L0_rec_W2': _L0_rec_in['W2'], 'L0_rec_b2': _L0_rec_in['b2'], 'L0_rec_W3': _L0_rec_in['W3'], 'L0_rec_b3': _L0_rec_in['b3'], 'L0_rec_deep_w': _L0_rec_in['deep_w'], 'L0_rec_deep_b': _L0_rec_in['deep_b'], 'L0_rec_bias': _L0_rec_in['bias']}

def reference(r_dense, r_sparse, L0_rec_tables, L0_rec_lin_sparse_w, L0_rec_lin_dense_w, L0_rec_conv1_w, L0_rec_conv1_b, L0_rec_conv2_w, L0_rec_conv2_b, L0_rec_cin_w, L0_rec_cin_b, L0_rec_W1, L0_rec_b1, L0_rec_W2, L0_rec_b2, L0_rec_W3, L0_rec_b3, L0_rec_deep_w, L0_rec_deep_b, L0_rec_bias):
    import jax
    import jax.numpy as jnp

    def _L0_rec_ref(sparse, dense, tables, lin_sparse_w, lin_dense_w, conv1_w, conv1_b, conv2_w, conv2_b, cin_w, cin_b, W1, b1, W2, b2, W3, b3, deep_w, deep_b, bias):
        import jax, jax.numpy as jnp
        import numpy as np
        B, M, V, E, ND = (512, 26, 1250, 32, 13)
        CIN_LAYERS = (128, 128)
        DEEP = (1024, 512, 256)
        DEEP_IN = M * E + ND
        CIN_CORES = sum((h - h // 2 for h in CIN_LAYERS))

        def _xdeepfm(sparse, dense, tables, lin_sparse_w, lin_dense_w, conv1_w, conv1_b, conv2_w, conv2_b, cin_w, cin_b, W1, b1, W2, b2, W3, b3, deep_w, deep_b, bias):
            feat_idx = jnp.arange(M)
            emb = tables[feat_idx, sparse]
            linear_out = lin_sparse_w[feat_idx, sparse].sum(-1) + dense @ lin_dense_w
            x0 = emb
            xk = emb
            res = []
            for w, bb in ((conv1_w, conv1_b), (conv2_w, conv2_b)):
                h = xk.shape[1]
                hp = jnp.einsum('bhd,bmd->bhmd', xk, x0).reshape(-1, h * M, E)
                xn = jax.nn.sigmoid(jnp.einsum('oi,bid->bod', w, hp) + bb[None, :, None])
                half = xn.shape[1] // 2
                xk = xn[:, :half]
                res.append(xn[:, half:])
            cin_feat = jnp.concatenate(res, axis=1).sum(-1)
            cin_out = (cin_feat @ cin_w + cin_b)[:, 0]
            deep_x = jnp.concatenate([emb.reshape(-1, M * E), dense], axis=-1)
            h1 = jnp.tanh(deep_x @ W1 + b1)
            h2 = jnp.tanh(h1 @ W2 + b2)
            h3 = jnp.tanh(h2 @ W3 + b3)
            deep_out = (h3 @ deep_w + deep_b)[:, 0]
            return linear_out + cin_out + deep_out + bias[0]
        return _xdeepfm(sparse, dense, tables, lin_sparse_w, lin_dense_w, conv1_w, conv1_b, conv2_w, conv2_b, cin_w, cin_b, W1, b1, W2, b2, W3, b3, deep_w, deep_b, bias)
    y = _L0_rec_ref(r_sparse, r_dense, L0_rec_tables, L0_rec_lin_sparse_w, L0_rec_lin_dense_w, L0_rec_conv1_w, L0_rec_conv1_b, L0_rec_conv2_w, L0_rec_conv2_b, L0_rec_cin_w, L0_rec_cin_b, L0_rec_W1, L0_rec_b1, L0_rec_W2, L0_rec_b2, L0_rec_W3, L0_rec_b3, L0_rec_deep_w, L0_rec_deep_b, L0_rec_bias)
    return y

_drawn_inputs = setup_inputs


def setup_inputs(seed=0):
    import zlib

    import numpy as np

    out = dict(_drawn_inputs(seed))
    spreads = {'L0_rec_conv1_b': (0.0, 0.408),
     'L0_rec_conv2_b': (0.0, 0.344),
     'L0_rec_b1': (0.0, 0.8),
     'L0_rec_b2': (0.0, 0.8),
     'L0_rec_b3': (0.0, 0.8)}
    factors = {'r_dense': 3.433,
     'L0_rec_tables': 8.0,
     'L0_rec_lin_sparse_w': 4.042,
     'L0_rec_lin_dense_w': 4.359,
     'L0_rec_conv1_w': 8.0,
     'L0_rec_conv2_w': 8.0,
     'L0_rec_W1': 2.692,
     'L0_rec_W3': 3.826,
     'L0_rec_deep_w': 2.855}
    for name, (base, spread) in spreads.items():
        noise = np.random.default_rng([zlib.crc32(name.encode()), seed]).standard_normal(out[name].shape)
        drawn = base * np.exp(spread * noise) if base else spread * noise
        out[name] = jnp.asarray(drawn.astype(out[name].dtype))
    for name, factor in factors.items():
        out[name] = (out[name] * factor).astype(out[name].dtype)
    return out
```

```python
from contextlib import ExitStack

import numpy as np

import concourse.bass as bass
from concourse import mybir

F32 = mybir.dt.float32
BF16 = mybir.dt.bfloat16
I32 = mybir.dt.int32
ALU = mybir.AluOpType
ACT = mybir.ActivationFunctionType
AX_X = mybir.AxisListType.X

P = 128
B, M, V, D, ND = 2048, 26, 1250, 32, 13
ROW = D + 1
TILES = B // P
STEP_D = 8
STEPS = D // STEP_D
COLS = STEP_D * P
CHUNK = 512
H = 64
PARTS = 3
PM = PARTS * M
PAIRS = M // 2
K1 = 3
F1N, F2N, F3N = 1024, 512, 256
KD = 7
DEEP_ROWS = M * ROW + ND
LAST_E = M * ROW - (KD - 1) * P
LAST_K = LAST_E + ND
GROUPS = B // CHUNK
HP_SLOTS = 4

UNITS = [0, 1, 2, 3, 4, "A", 5, ("K", 0), 6, ("K", 1), 7, ("K", 2), 8, 9, 10, 11, 12]
UNITS_LAST = list(range(PAIRS))
N_UNITS = len(UNITS)
BY_DMA = [1, 3, 6, 7, 9, 11]
N_SPREADS = N_UNITS - len(BY_DMA)
XB_SLOTS = 3
PER_SLOT = len(BY_DMA) // XB_SLOTS
N_PRODUCTS = PAIRS + K1
POS_A = UNITS.index("A")
PROLOGUE_UNITS = 1 + K1


def pair_rows():
    rows = [(k, p) for k in range(K1) for p in range(P)]
    free = {h: [r for r in rows if r[1] % M == h] for h in range(M)}
    second = {}
    for h in range(M):
        for gap in range(M // 2 + 1):
            m = (h + gap) % M
            if gap == M // 2 and h > m:
                continue
            own, other = (h, m) if free[h] else (m, h)
            second[free[own].pop(0)] = other
    assert len(second) == M * (M + 1) // 2
    return second


def is_product(unit):
    return unit != "A"


def products_before(units, pos):
    return sum(is_product(u) for u in units[:pos])


def is_spread(unit):
    return unit not in BY_DMA


def spreads_before(units, pos):
    return sum(is_spread(u) for u in units[:pos])


def build(nc, table, sparse, dense_t, lin_dense, pair_a, pair_b, w2rows, conv1_b, conv2_b, cin_w,
          scalars, W1, b1, W2, b2, W3, b3, deep_w, sel_first, sel_second, sel_pair, ident_b, ident_f,
          out):
    with ExitStack() as ctx:
        def sb(name, shape, dt=F32):
            return ctx.enter_context(nc.sbuf_tensor(name, shape, dt))

        def pb(name, shape, dt=F32):
            return ctx.enter_context(nc.psum_tensor(name, shape, dt))

        def sem(name):
            return ctx.enter_context(nc.semaphore(name))

        idx_all = sb("idx_all", [P, TILES, M], I32)
        idx_stage = sb("idx_stage", [P, M], I32)
        idb = sb("idb", [P, P], BF16)
        idf = sb("idf", [P, P])
        selA = sb("selA", [PM, P], BF16)
        selK = sb("selK", [PM, K1, P], BF16)
        selJ = sb("selJ", [PM, PAIRS, P], BF16)
        w1s = sb("w1s", [P, K1, P])
        w2s = sb("w2s", [P, PAIRS, H])
        bias1 = sb("bias1", [P, 1])
        bias2 = sb("bias2", [P, 1])
        wd1 = sb("wd1", [P, KD, F1N])
        wd2 = sb("wd2", [P, F1N // P, F2N])
        wd3 = sb("wd3", [P, F2N // P, F3N])
        bd1 = sb("bd1", [P, F1N // P])
        bd2 = sb("bd2", [P, F2N // P])
        bd3 = sb("bd3", [P, F3N // P])
        wdo = sb("wdo", [P, F3N // P])
        cw1 = sb("cw1", [H + ND, 1])
        cw2 = sb("cw2", [P, 1])
        sc3 = sb("sc3", [P, 3])
        bias_out = sb("bias_out", [P, 1])
        emb = sb("emb", [P, M, ROW])
        rem = sb("rem", [P, M, D])
        parts = sb("parts", [P, D, PM], BF16)
        deep_t = sb("deep_t", [P, KD, B])
        x0t = [sb(f"x0t{i}", [PM, COLS], BF16) for i in range(2)]
        first_both = sb("first_both", [P, 2, COLS])
        first = [first_both[:, i, :] for i in range(2)]
        xk_both = sb("xk_both", [P, 2, COLS])
        xk = [xk_both[:, i, :] for i in range(2)]
        r1_both = sb("r1_both", [P, 2, COLS])
        r1 = [r1_both[0:H, i, :] for i in range(2)]
        r2 = [sb(f"r2_{i}", [P, CHUNK]) for i in range(2)]
        hp_all = sb("hp_all", [P, HP_SLOTS, COLS])
        hp = [hp_all[:, i, :] for i in range(HP_SLOTS)]
        xb = [sb(f"xb{i}", [P, COLS]) for i in range(XB_SLOTS)]
        rows = nc.dram_tensor("x0_rows", (2, M, COLS), F32, kind="Internal").ap()
        sum1 = sb("sum1", [H + ND, B])
        sum2 = sb("sum2", [P, B])
        IDX_N = TILES * M

        def at_start(n, first_col, shape):
            return sum2[:, first_col:first_col + n].rearrange(shape[0], **shape[1])

        raw_idx = at_start(IDX_N, 0, ("p (t m) -> p t m", {"m": M})).bitcast(I32)
        field_base = at_start(IDX_N, IDX_N, ("p (t m) -> p t m", {"m": M})).bitcast(I32)
        wrapped = at_start(IDX_N, 2 * IDX_N, ("p (t m) -> p t m", {"m": M}))
        w1a = at_start(K1 * P, 3 * IDX_N, ("p (k o) -> p k o", {"k": K1}))
        w1b = at_start(K1 * P, 3 * IDX_N + K1 * P, ("p (k o) -> p k o", {"k": K1}))
        tmp1 = sb("tmp1", [H, P])
        tmp2 = sb("tmp2", [P, P])
        lin_sum = sb("lin_sum", [P, TILES])
        h1 = hp_all[:, :, :].rearrange("p s (a n) -> p (s a) n", n=CHUNK)
        h2 = xk_both[:, :, :].rearrange("p s (a n) -> p (s a) n", n=CHUNK)
        h3 = [both[:, :, :].rearrange("p s n -> p (s n)") for both in (first_both, r1_both)]
        orow = r2[0][:, :]

        bc = [pb(f"bc{i}", [P, COLS]) for i in range(2)]
        xn = pb("xn", [P, COLS])
        y2 = pb("y2", [P, CHUNK])
        tr = pb("tr", [P, CHUNK])
        tr_b = tr[:, :].bitcast(BF16)

        idx_loaded = sem("idx_loaded")
        sel_loaded = sem("sel_loaded")
        w1_loaded = sem("w1_loaded")
        w2_loaded = sem("w2_loaded")
        deep_loaded = sem("deep_loaded")
        end_loaded = sem("end_loaded")
        iota_done = sem("iota_done")
        idx_step = sem("idx_step")
        w1_summed = sem("w1_summed")
        bias_summed = sem("bias_summed")
        idx_staged = sem("idx_staged")
        pool_held = sem("pool_held")
        sp_held = sem("sp_held")
        gathered = sem("gathered")
        split = sem("split")
        lin_done = sem("lin_done")
        x0t_turned = sem("x0t_turned")
        x0t_copied = sem("x0t_copied")
        deep_turned = sem("deep_turned")
        deep_copied = sem("deep_copied")
        spread = sem("spread")
        first_copied = sem("first_copied")
        rows_written = sem("rows_written")
        filled = [sem(f"filled{i}") for i in range(XB_SLOTS)]
        multiplied = sem("multiplied")
        contracted = sem("contracted")
        xn_read = sem("xn_read")
        y2_read = sem("y2_read")
        r1_reduced = sem("r1_reduced")
        r1_added = sem("r1_added")
        r2_reduced = sem("r2_reduced")
        r2_added = sem("r2_added")
        acc_ready = sem("acc_ready")
        act_done = sem("act_done")
        out_ready = sem("out_ready")
        row_ready = sem("row_ready")
        stored = sem("stored")

        def spread_by(s, pos, units=UNITS):
            return s * N_SPREADS + (PROLOGUE_UNITS + spreads_before(units, pos + 1))

        def bc_slot(sl, units, pos):
            return (sl * N_SPREADS + spreads_before(units, pos)) % 2

        def product_by(s, pos, units=UNITS):
            return s * N_PRODUCTS + (K1 + products_before(units, pos + 1))

        def products_through(s):
            return s * N_PRODUCTS + K1

        SPLITS = 4
        GATHERED = 16 * M

        def over_tiles(eng, tile):
            tile(0, True, False)
            with eng.Fori(1, TILES - 1) as t:
                tile(t, False, False)
            tile(TILES - 1, False, True)

        block = ctx.enter_context(nc.Block())

        @block.sync
        def _(sp):
            sp.dma_start(raw_idx[:, :, :], sparse.rearrange("(t p) m -> p t m", p=P)).then_inc(idx_loaded, 16)
            for dst, src in ((idb[:, :], ident_b), (selA[:, :], sel_first),
                             (selK[:, :, :], sel_second), (selJ[:, :, :], sel_pair)):
                sp.dma_start(dst, src).then_inc(sel_loaded, 16)
            for dst, src in ((w1a[:, :, :], pair_a), (w1b[:, :, :], pair_b),
                             (bias1[:, :], conv1_b.rearrange("(p o) -> p o", o=1))):
                sp.dma_start(dst, src).then_inc(w1_loaded, 16)
            sp.dma_start(w2s[:, :, :], w2rows).then_inc(w2_loaded, 16)
            for c in range(2):
                sp.dma_start(bias2[H * c:H * c + H, :], conv2_b[H:2 * H].rearrange("(p o) -> p o", o=1)).then_inc(w2_loaded, 16)
            for dst, src in ((idf[:, :], ident_f),
                             (deep_t[LAST_E:LAST_K, KD - 1, :], dense_t),
                             (wd1[:, 0:KD - 1, :], W1[0:(KD - 1) * P, :].rearrange("(k p) n -> p k n", p=P)),
                             (wd1[0:LAST_K, KD - 1, :], W1[(KD - 1) * P:DEEP_ROWS, :]),
                             (wd2[:, :, :], W2.rearrange("(k p) n -> p k n", p=P)),
                             (wd3[:, :, :], W3.rearrange("(k p) n -> p k n", p=P)),
                             (bd1[:, :], b1),
                             (bd2[:, :], b2),
                             (bd3[:, :], b3)):
                sp.dma_start(dst, src).then_inc(deep_loaded, 16)
            for dst, src in ((wdo[:, :], deep_w),
                             (cw1[0:H, :], cin_w[0:H, :]), (cw2[0:H, :], cin_w[H:2 * H, :]),
                             (cw2[H:P, :], cin_w[H:2 * H, :]),
                             (cw1[H:H + ND, :], lin_dense.rearrange("(p o) -> p o", o=1)),
                             (sum1[H:H + ND, :], dense_t), (sc3[:, :], scalars)):
                sp.dma_start(dst, src).then_inc(end_loaded, 16)
            def hold():
                sp.sem_inc(sp_held, 1)

            def write_rows(s, sl):
                sp.wait_ge(first_copied, s + 1)
                hold()
                sp.dma_start(rows[sl % 2, :, :], first[sl % 2][0:M, :]).then_inc(rows_written, 16)

            def fill(s, sl, n, is_first):
                u, slot = BY_DMA[n], n % XB_SLOTS
                if n == 0:
                    sp.wait_ge(rows_written, s * 16 + 16)
                    hold()
                before = BY_DMA[n - XB_SLOTS]
                if n >= XB_SLOTS:
                    sp.wait_ge(multiplied, product_by(s, UNITS.index(before)))
                    hold()
                elif not is_first:
                    sp.wait_ge(multiplied, product_by(s - 1, UNITS.index(before)))
                    hold()
                sp.dma_start(xb[slot][:, :], rows[sl % 2, 2 * u:2 * u + 2, :].unsqueeze(1).to_broadcast([2, H, COLS])
                             ).then_inc(filled[slot], 16)

            write_rows(0, 0)
            for n in range(XB_SLOTS):
                fill(0, 0, n, True)

            def tile(t, is_first, is_last):
                for sl in range(STEPS):
                    s = t * STEPS + sl
                    final = is_last and sl == STEPS - 1
                    for n in range(XB_SLOTS, len(BY_DMA)):
                        u = BY_DMA[n - XB_SLOTS]
                        if final:
                            sp.wait_ge(multiplied, product_by(s, UNITS_LAST.index(u), UNITS_LAST))
                            hold()
                            sp.dma_start(xb[n % XB_SLOTS][:, :],
                                         rows[sl % 2, 2 * BY_DMA[n]:2 * BY_DMA[n] + 2, :].unsqueeze(1).to_broadcast([2, H, COLS])
                                         ).then_inc(filled[n % XB_SLOTS], 16)
                        else:
                            fill(s, sl, n, False)
                    if final:
                        continue
                    for slot in range(XB_SLOTS):
                        sp.wait_ge(filled[slot], s * (16 * PER_SLOT) + 16 * PER_SLOT)
                        hold()
                    write_rows(s + 1, sl + 1)
                    for n in range(XB_SLOTS):
                        fill(s + 1, sl + 1, n, False)

            over_tiles(sp, tile)
            sp.wait_ge(row_ready, GROUPS)
            sp.dma_start(out.rearrange("(g n) -> g n", n=CHUNK),
                         orow[0:32 * (GROUPS - 1) + 1:32, :]).then_inc(stored, 16)
            sp.wait_ge(stored, 16)

        SEL_LOADED, W1_LOADED, W2_LOADED, DEEP_LOADED, END_LOADED = 64, 48, 48, 144, 112

        @block.gpsimd
        def _(pool):
            nc.gpsimd.iota(field_base[:, :, :], [[0, TILES], [V, M]], base=0, channel_multiplier=0).then_inc(iota_done, 1)

            def hold():
                pool.sem_inc(pool_held, 1)

            def gather(t):
                hold()
                nc.gpsimd.tensor_copy(idx_stage[:, :], idx_all[:, bass.ds(t, 1), :].rearrange("p a m -> p (a m)")).then_inc(idx_staged, 1)
                pool.wait_ge(idx_staged, t + 1)
                hold()
                for m in range(M):
                    nc.gpsimd.indirect_dma_start(
                        out=emb[:, m, :], out_offset=None, in_=table,
                        in_offset=bass.IndirectOffsetOnAxis(ap=idx_stage[:, m:m + 1], axis=0)).then_inc(gathered, 16)

            def split_parts(t):
                def part(i):
                    return parts[:, :, i * M:(i + 1) * M].rearrange("p d m -> p m d")

                pool.wait_ge(gathered, t * GATHERED + GATHERED)
                hold()
                nc.gpsimd.tensor_copy(part(0), emb[:, :, 0:D]).then_inc(split, 1)
                pool.wait_ge(split, t * SPLITS + 1)
                nc.gpsimd.tensor_tensor(rem[:, :, :], emb[:, :, 0:D], part(0), ALU.subtract).then_inc(split, 1)
                pool.wait_ge(split, t * SPLITS + 2)
                hold()
                nc.gpsimd.tensor_copy(part(1), rem[:, :, :]).then_inc(split, 1)
                pool.wait_ge(split, t * SPLITS + 3)
                nc.gpsimd.tensor_tensor(part(2), rem[:, :, :], part(1), ALU.subtract).then_inc(split, 1)

            pool.wait_ge(idx_step, 4)
            gather(0)
            split_parts(0)

            def next_tile(t):
                pool.wait_ge(split, t * SPLITS + SPLITS)
                pool.wait_ge(deep_turned, t * 2 + 2)
                pool.wait_ge(lin_done, t + 1)
                gather(t + 1)
                pool.wait_ge(x0t_turned, t * STEPS + STEPS)
                split_parts(t + 1)

            with pool.Fori(0, TILES - 1) as t:
                next_tile(t)

        @block.vector
        def _(dve):
            dve.wait_ge(idx_loaded, 16)
            nc.vector.tensor_scalar(wrapped[:, :, :], raw_idx[:, :, :], 0.0, float(V), ALU.is_lt, ALU.mult).then_inc(idx_step, 1)
            dve.wait_ge(idx_step, 1)
            nc.vector.tensor_tensor(wrapped[:, :, :], wrapped[:, :, :], raw_idx[:, :, :], ALU.add).then_inc(idx_step, 1)
            dve.wait_ge(idx_step, 2)
            nc.vector.tensor_scalar(wrapped[:, :, :], wrapped[:, :, :], 0.0, float(V - 1), ALU.max, ALU.min).then_inc(idx_step, 1)
            dve.wait_ge(idx_step, 3)
            dve.wait_ge(iota_done, 1)
            nc.vector.tensor_tensor(idx_all[:, :, :], wrapped[:, :, :], field_base[:, :, :], ALU.add).then_inc(idx_step, 1)
            dve.wait_ge(w1_loaded, W1_LOADED)
            nc.vector.tensor_tensor(w1s[:, :, :], w1a[:, :, :], w1b[:, :, :], ALU.add).then_inc(w1_summed, 1)
            dve.wait_ge(end_loaded, END_LOADED)
            nc.vector.tensor_reduce(bias_out[:, :], sc3[:, :], AX_X, ALU.add).then_inc(bias_summed, 1)

            def product(number, spread_rows, other):
                n, local = number
                if local >= HP_SLOTS or not isinstance(n, int):
                    dve.wait_ge(contracted, n - HP_SLOTS + 1)
                nc.vector.tensor_tensor(hp[local % HP_SLOTS][:, :], spread_rows, other, ALU.mult).then_inc(multiplied, 1)

            dve.wait_ge(first_copied, 1)
            for k in range(K1):
                dve.wait_ge(spread, 2 + k)
                product((k, k), bc[(1 + k) % 2][:, :], first[0][:, :])

            def reduce_r1(t, sl):
                s = t * STEPS + sl
                dve.wait_ge(xn_read, s + 1)
                if sl > 0:
                    if sl > 1 or not isinstance(t, int) or t > 0:
                        dve.wait_ge(r1_added, t * (STEPS - 1) + (sl - 1))
                    dst = tmp1[:, :]
                else:
                    dst = sum1[0:H, bass.ds(t * P, P)]
                nc.vector.tensor_reduce(dst, r1[sl % 2][:, :].rearrange("p (q b) -> p b q", b=P), AX_X, ALU.add).then_inc(r1_reduced, 1)

            def add_r1(t, sl):
                dve.wait_ge(r1_reduced, t * STEPS + (sl + 1))
                acc = sum1[0:H, bass.ds(t * P, P)]
                nc.vector.tensor_tensor(acc, acc, tmp1[:, :], ALU.add).then_inc(r1_added, 1)

            def reduce_r2(t, sl):
                s = t * STEPS + sl
                dve.wait_ge(y2_read, s + 1)
                if sl > 0:
                    if sl > 1 or not isinstance(t, int) or t > 0:
                        dve.wait_ge(r2_added, t * (STEPS - 1) + (sl - 1))
                    dst = tmp2[:, :]
                else:
                    dst = sum2[:, bass.ds(t * P, P)]
                nc.vector.tensor_reduce(dst, r2[sl % 2][:, :].rearrange("p (q b) -> p b q", b=P), AX_X, ALU.add).then_inc(r2_reduced, 1)

            def add_r2(t, sl):
                dve.wait_ge(r2_reduced, t * STEPS + (sl + 1))
                acc = sum2[:, bass.ds(t * P, P)]
                nc.vector.tensor_tensor(acc, acc, tmp2[:, :], ALU.add).then_inc(r2_added, 1)

            def tile(t, is_first, is_last):
                for sl in range(STEPS):
                    s = t * STEPS + sl
                    units = UNITS_LAST if is_last and sl == STEPS - 1 else UNITS
                    before = (t, sl - 1) if sl else (t - 1, STEPS - 1)
                    has_before = not (is_first and sl == 0)
                    dve.wait_ge(xn_read, s + 1)
                    for pos, unit in enumerate(units):
                        if unit == "A":
                            continue
                        if unit == ("K", 0):
                            dve.wait_ge(first_copied, s + 2)
                        other = xk[sl % 2] if isinstance(unit, int) else first[(sl + 1) % 2]
                        local = K1 + products_before(units, pos)
                        if is_spread(unit):
                            dve.wait_ge(spread, spread_by(s, pos, units))
                            spread_rows = bc[bc_slot(sl, units, pos)]
                        else:
                            n = BY_DMA.index(unit)
                            spread_rows = xb[n % XB_SLOTS]
                            dve.wait_ge(filled[n % XB_SLOTS], s * (16 * PER_SLOT) + 16 * (n // XB_SLOTS + 1))
                        product((s * N_PRODUCTS + local, local + (0 if is_first and sl == 0 else HP_SLOTS)),
                                spread_rows[:, :], other[:, :])
                        if pos == 1:
                            reduce_r1(t, sl)
                        if pos == 3 and sl:
                            add_r1(t, sl)
                        if pos == 6 and has_before:
                            reduce_r2(*before)
                        if pos == 8 and has_before and before[1]:
                            add_r2(*before)
                        if pos == 9 and sl == 0:
                            dve.wait_ge(gathered, t * GATHERED + GATHERED)
                            nc.vector.tensor_reduce(lin_sum[:, bass.ds(t, 1)], emb[:, :, D], AX_X, ALU.add).then_inc(lin_done, 1)

            over_tiles(dve, tile)
            reduce_r2(TILES - 1, STEPS - 1)
            add_r2(TILES - 1, STEPS - 1)

        N_ACC = (F1N + F2N + F3N) // P
        LAST_PRODUCT = product_by(TILES * STEPS - 1, PAIRS - 1, UNITS_LAST)

        @block.tensor
        def _(pe):
            def turn_x0(t, sl):
                for q in range(STEP_D):
                    last = nc.tensor.transpose(tr_b[0:PM, q * P:(q + 1) * P], parts[:, sl * STEP_D + q, :], idb[:, :])
                last.then_inc(x0t_turned, 1)

            def turn_deep(ks):
                numbers = emb[:, :, :].rearrange("p m e -> p (m e)")
                for i, k in enumerate(ks):
                    n = min(P, M * ROW - k * P)
                    last = nc.tensor.transpose(tr[0:n, i * P:(i + 1) * P], numbers[:, k * P:k * P + n], idf[:, :])
                last.then_inc(deep_turned, 1)

            def broadcast(unit, slot, sl):
                x = x0t[sl % 2] if isinstance(unit, int) else x0t[(sl + 1) % 2]
                sel = selJ[:, unit, :] if isinstance(unit, int) else selA[:, :] if unit == "A" else selK[:, unit[1], :]
                for c in range(2):
                    last = nc.tensor.matmul(bc[slot][:, c * CHUNK:(c + 1) * CHUNK], sel, x[:, c * CHUNK:(c + 1) * CHUNK],
                                            start=True, stop=True)
                last.then_inc(spread, 1)

            def contract(unit, slot):
                for c in range(2):
                    src = hp[slot][:, c * CHUNK:(c + 1) * CHUNK]
                    if isinstance(unit, int):
                        last = nc.tensor.matmul(y2[H * c:H * c + H, :], w2s[:, unit, :], src,
                                                start=(unit == 0), stop=(unit == PAIRS - 1))
                    else:
                        last = nc.tensor.matmul(xn[:, c * CHUNK:(c + 1) * CHUNK], w1s[:, unit[1], :], src,
                                                start=(unit[1] == 0), stop=(unit[1] == K1 - 1))
                last.then_inc(contracted, 1)

            pe.wait_ge(sel_loaded, SEL_LOADED)
            pe.wait_ge(split, SPLITS)
            turn_x0(0, 0)
            pe.wait_ge(x0t_copied, 1)
            broadcast("A", 0, -1)
            broadcast(("K", 0), 1, -1)
            pe.wait_ge(first_copied, 1)
            broadcast(("K", 1), 0, -1)
            pe.wait_ge(w1_summed, 1)
            for k in range(K1):
                pe.wait_ge(multiplied, k + 1)
                if k == 0:
                    broadcast(("K", 2), 1, -1)
                contract(("K", k), k % HP_SLOTS)
            pe.wait_ge(w2_loaded, W2_LOADED)
            pe.wait_ge(deep_loaded, DEEP_LOADED)

            def tile(t, is_first, is_last):
                def contract_unit(units, s, pos):
                    unit = units[pos]
                    if not is_product(unit):
                        return
                    pe.wait_ge(multiplied, product_by(s, pos, units))
                    if unit == 0 and not (isinstance(s, int) and s == 0):
                        pe.wait_ge(y2_read, s)
                    if unit == ("K", 0):
                        pe.wait_ge(xn_read, s + 1)
                    contract(unit, (K1 + products_before(units, pos)) % HP_SLOTS)

                for sl in range(STEPS):
                    s = t * STEPS + sl
                    final = is_last and sl == STEPS - 1
                    units = UNITS_LAST if final else UNITS
                    for pos, unit in enumerate(units):
                        if pos == 0:
                            pe.wait_ge(x0t_copied, s + 1)
                        if unit == "A":
                            pe.wait_ge(x0t_copied, s + 2)
                        if is_spread(unit):
                            earlier = [q for q in range(pos) if is_spread(units[q])]
                            if len(earlier) >= 2:
                                q = earlier[-2]
                                if units[q] == "A":
                                    pe.wait_ge(first_copied, s + 2)
                                else:
                                    pe.wait_ge(multiplied, product_by(s, q, units))
                            elif is_first and sl == 0:
                                pe.wait_ge(multiplied, K1 - 1 + len(earlier))
                            else:
                                q = [q for q in range(N_UNITS) if is_spread(UNITS[q])][len(earlier) - 2]
                                pe.wait_ge(multiplied, product_by(s - 1, q))
                            broadcast(unit, bc_slot(sl, units, pos), sl)
                        if pos == 2 and not final:
                            if sl == STEPS - 1:
                                pe.wait_ge(split, t * SPLITS + 2 * SPLITS)
                                turn_x0(t + 1, 0)
                            else:
                                if sl == 1:
                                    pe.wait_ge(deep_copied, t * 2 + 2)
                                turn_x0(t, sl + 1)
                        if sl == 0 and pos == 6:
                            pe.wait_ge(gathered, t * GATHERED + GATHERED)
                            pe.wait_ge(x0t_copied, s + 2)
                            turn_deep(range(4))
                        if sl == 0 and pos == 10:
                            pe.wait_ge(deep_copied, t * 2 + 1)
                            turn_deep(range(4, KD))
                        if pos >= 2:
                            contract_unit(units, s, pos - 2)
                        elif not (is_first and sl == 0):
                            contract_unit(UNITS, s - 1, N_UNITS - 2 + pos)
                if is_last:
                    for pos in range(PAIRS - 2, PAIRS):
                        contract_unit(UNITS_LAST, TILES * STEPS - 1, pos)

            over_tiles(pe, tile)

            def deep_group(g, is_first):
                cols = bass.ds(g * CHUNK, CHUNK)
                base = g * N_ACC

                def layer(at, tiles, weights, rows, rhs, inputs):
                    for m in range(tiles):
                        a = at + m
                        if not (is_first and a < 2):
                            pe.wait_ge(act_done, base + (a - 1))
                        for k in range(rows):
                            if m == 0 and inputs is not None:
                                pe.wait_ge(act_done, base + (inputs + k + 1))
                            kp = LAST_K if inputs is None and k == rows - 1 else P
                            last = nc.tensor.matmul(bc[a % 2][:, 0:CHUNK], weights[0:kp, k, m * P:(m + 1) * P],
                                                    rhs(k, kp), start=(k == 0), stop=(k == rows - 1))
                        last.then_inc(acc_ready, 1)

                layer(0, F1N // P, wd1, KD, lambda k, kp: deep_t[0:kp, k, cols], None)
                layer(F1N // P, F2N // P, wd2, F1N // P, lambda k, kp: h1[:, k, :], 0)
                layer((F1N + F2N) // P, F3N // P, wd3, F2N // P, lambda k, kp: h2[:, k, :], F1N // P)

            pe.wait_ge(multiplied, LAST_PRODUCT)
            pe.wait_ge(deep_copied, 2 * TILES)
            deep_group(0, True)
            with pe.Fori(1, GROUPS) as g:
                deep_group(g, False)

            pe.wait_ge(end_loaded, END_LOADED)
            pe.wait_ge(xn_read, TILES * STEPS)
            pe.wait_ge(r1_reduced, TILES * STEPS)
            pe.wait_ge(r1_added, TILES * (STEPS - 1))
            pe.wait_ge(r2_added, TILES * (STEPS - 1))
            pe.wait_ge(lin_done, TILES)
            terms = [(cw1[:, :], sum1[:, :]), (cw2[:, :], sum2[:, :])]
            terms += [(wdo[:, k:k + 1], h3[k]) for k in range(F3N // P)]
            for n, (w, x) in enumerate(terms):
                if n == 2:
                    pe.wait_ge(act_done, GROUPS * N_ACC)
                for g in range(GROUPS):
                    nc.tensor.matmul(xn[32 * g:32 * g + 1, 0:CHUNK], w, x[:, g * CHUNK:(g + 1) * CHUNK],
                                     start=(n == 0), stop=False, skip_group_check=True)
            for c in range(CHUNK // P):
                for g in range(GROUPS):
                    t = g * (CHUNK // P) + c
                    last = nc.tensor.matmul(xn[32 * g:32 * g + 1, c * P:(c + 1) * P], lin_sum[:, t:t + 1], idf[:, :],
                                            start=False, stop=True, skip_group_check=True)
            last.then_inc(out_ready, 1)

        @block.scalar
        def _(act):
            act.wait_ge(w1_loaded, W1_LOADED)

            def copy_x0(s, sl):
                act.wait_ge(x0t_turned, s + 1)
                nc.scalar.activation(x0t[sl % 2][:, :], tr_b[0:PM, :], ACT.Copy).then_inc(x0t_copied, 1)

            def read_xn(slot):
                nc.scalar.activation(xk[slot][0:H, :], xn[0:H, :], ACT.Sigmoid, bias=bias1[0:H, :])
                nc.scalar.activation(xk[slot][H:P, :], xn[0:H, :], ACT.Sigmoid, bias=bias1[0:H, :])
                nc.scalar.activation(r1[slot][:, :], xn[H:P, :], ACT.Sigmoid, bias=bias1[H:P, :]).then_inc(xn_read, 1)

            def read_y2(s, slot, count, is_early):
                act.wait_ge(contracted, count)
                if not is_early:
                    act.wait_ge(r2_reduced, s - 1)
                nc.scalar.activation(r2[slot][:, :], y2[:, :], ACT.Sigmoid, bias=bias2[:, :]).then_inc(y2_read, 1)

            copy_x0(0, 0)
            act.wait_ge(spread, 1)
            nc.scalar.activation(first[0][:, :], bc[0][:, :], ACT.Copy).then_inc(first_copied, 1)
            act.wait_ge(contracted, K1)
            read_xn(0)
            act.wait_ge(w2_loaded, W2_LOADED)

            def tile(t, is_first, is_last):
                for sl in range(STEPS):
                    s = t * STEPS + sl
                    start = is_first and sl == 0
                    if not start:
                        read_y2(s - 1, (sl + 1) % 2, products_through(s), is_first and sl <= 2)
                    if is_last and sl == STEPS - 1:
                        continue
                    act.wait_ge(spread, s * N_SPREADS + PROLOGUE_UNITS)
                    copy_x0(s + 1, sl + 1)
                    act.wait_ge(spread, spread_by(s, POS_A))
                    if not start:
                        act.wait_ge(multiplied, products_through(s - 1) if not (is_first and sl == 1) else K1)
                        act.wait_ge(rows_written, s * 16)
                    slot = bc_slot(sl, UNITS, POS_A)
                    nc.scalar.activation(first[(sl + 1) % 2][:, :], bc[slot][:, :], ACT.Copy).then_inc(first_copied, 1)
                    if sl == 0:
                        for half in range(2):
                            act.wait_ge(deep_turned, t * 2 + (half + 1))
                            cols = bass.ds(t * P, P)
                            if half == 0:
                                nc.scalar.activation(deep_t[:, 0:4, cols], tr[:, :].rearrange("p (k b) -> p k b", b=P),
                                                     ACT.Copy).then_inc(deep_copied, 1)
                            else:
                                nc.scalar.activation(deep_t[:, 4:6, cols], tr[:, 0:2 * P].rearrange("p (k b) -> p k b", b=P), ACT.Copy)
                                nc.scalar.activation(deep_t[0:LAST_E, 6, cols], tr[0:LAST_E, 2 * P:3 * P],
                                                     ACT.Copy).then_inc(deep_copied, 1)
                    act.wait_ge(contracted, product_by(s, UNITS.index(("K", K1 - 1))))
                    if not start:
                        act.wait_ge(multiplied, products_through(s))
                        act.wait_ge(r1_reduced, s)
                    read_xn((sl + 1) % 2)

            over_tiles(act, tile)
            read_y2(TILES * STEPS - 1, (TILES * STEPS - 1) % 2, LAST_PRODUCT, False)

            def deep_group(g):
                base = g * N_ACC
                a = 0
                for tiles, bias, dst in ((F1N // P, bd1, h1), (F2N // P, bd2, h2), (F3N // P, bd3, None)):
                    for m in range(tiles):
                        act.wait_ge(acc_ready, base + (a + 1))
                        to = dst[:, m, :] if dst is not None else h3[m][:, bass.ds(g * CHUNK, CHUNK)]
                        nc.scalar.activation(to, bc[a % 2][:, 0:CHUNK], ACT.Tanh, bias=bias[:, m:m + 1]).then_inc(act_done, 1)
                        a += 1

            act.wait_ge(deep_loaded, DEEP_LOADED)
            act.wait_ge(r1_reduced, TILES * STEPS)
            with act.Fori(0, GROUPS) as g:
                deep_group(g)
            act.wait_ge(bias_summed, 1)
            act.wait_ge(out_ready, 1)
            for g in range(GROUPS):
                r = slice(32 * g, 32 * g + 1)
                nc.scalar.activation(orow[r, :], xn[r, 0:CHUNK], ACT.Identity, bias=bias_out[r, :]).then_inc(row_ready, 1)


def kernel(r_dense, r_sparse, L0_rec_tables, L0_rec_lin_sparse_w, L0_rec_lin_dense_w, L0_rec_conv1_w,
           L0_rec_conv1_b, L0_rec_conv2_w, L0_rec_conv2_b, L0_rec_cin_w, L0_rec_cin_b, L0_rec_W1, L0_rec_b1,
           L0_rec_W2, L0_rec_b2, L0_rec_W3, L0_rec_b3, L0_rec_deep_w, L0_rec_deep_b, L0_rec_bias):
    import concourse.bacc as _bacc
    from concourse import mybir as _mybir
    from concourse.bass_utils import run_bass_kernel_spmd as _run

    f = np.asarray
    table = np.concatenate([f(L0_rec_tables).reshape(M * V, D), f(L0_rec_lin_sparse_w).reshape(M * V, 1)], axis=1)
    w1t = np.concatenate([f(L0_rec_conv1_w).T, np.zeros((1, P), np.float32)])
    row_a = np.full((P, K1), M * M)
    row_b = np.full((P, K1), M * M)
    second = pair_rows()
    for (k, p), m in second.items():
        h = p % M
        row_a[p, k] = h * M + m
        if m != h:
            row_b[p, k] = m * M + h
    w2 = f(L0_rec_conv2_w)[H:].reshape(H, H, PAIRS, 2).transpose(3, 1, 2, 0).reshape(P, PAIRS, H)
    deep1 = np.zeros((DEEP_ROWS, F1N), np.float32)
    deep1[:M * ROW].reshape(M, ROW, F1N)[:, :D] = f(L0_rec_W1)[:M * D].reshape(M, D, F1N)
    deep1[M * ROW:] = f(L0_rec_W1)[M * D:]
    bf = _mybir.dt.np(_mybir.dt.bfloat16)
    sel_first = np.zeros((PARTS, M, P), bf)
    sel_second = np.zeros((PARTS, M, K1, P), bf)
    sel_pair = np.zeros((PARTS, M, PAIRS, P), bf)
    for p in range(P):
        sel_first[:, p % M, p] = 1
        for j in range(PAIRS):
            sel_pair[:, 2 * j + p // H, j, p] = 1
    for (k, p), m in second.items():
        sel_second[:, m, k, p] = 1

    ins = {
        "table": table, "sparse": f(r_sparse), "dense_t": f(r_dense).T, "lin_dense": f(L0_rec_lin_dense_w),
        "pair_a": w1t[row_a], "pair_b": w1t[row_b], "w2rows": w2, "conv1_b": f(L0_rec_conv1_b),
        "conv2_b": f(L0_rec_conv2_b), "cin_w": f(L0_rec_cin_w),
        "scalars": np.tile(np.concatenate([f(L0_rec_cin_b), f(L0_rec_deep_b), f(L0_rec_bias)]), (P, 1)),
        "W1": deep1, "b1": f(L0_rec_b1).reshape(-1, P).T, "W2": f(L0_rec_W2), "b2": f(L0_rec_b2).reshape(-1, P).T, "W3": f(L0_rec_W3),
        "b3": f(L0_rec_b3).reshape(-1, P).T, "deep_w": f(L0_rec_deep_w).reshape(-1, P).T,
        "sel_first": sel_first.reshape(PM, P), "sel_second": sel_second.reshape(PM, K1, P),
        "sel_pair": sel_pair.reshape(PM, PAIRS, P),
        "ident_b": np.eye(P, dtype=bf), "ident_f": np.eye(P, dtype=np.float32),
    }
    nc = _bacc.Bacc("TRN2", target_bir_lowering=False, num_devices=1)
    arrays, args = {}, []
    for name, a in ins.items():
        a = np.ascontiguousarray(a)
        arrays[name] = a
        args.append(nc.dram_tensor(name, a.shape, _mybir.dt.from_np(a.dtype), kind="ExternalInput").ap())
    args.append(nc.dram_tensor("result", (B,), _mybir.dt.float32, kind="ExternalOutput").ap())
    build(nc, *args)
    r = _run(nc, [arrays], core_ids=[0])
    return r.results[0]["result"]
```

```python
from contextlib import ExitStack

import numpy as np

import concourse.bass as bass
from concourse import mybir

F32 = mybir.dt.float32
F32R = mybir.dt.float32r
BF16 = mybir.dt.bfloat16
I32 = mybir.dt.int32
ALU = mybir.AluOpType
ACT = mybir.ActivationFunctionType
AX_X = mybir.AxisListType.X

P = 128
B, M, V, D, ND = 2048, 26, 1250, 32, 13
ROW = D + 1
TILES = B // P
STEP_D = 8
STEPS = D // STEP_D
COLS = STEP_D * P
CHUNK = 512
H = 64
PARTS = 3
PM = PARTS * M
PAIRS = M // 2
K1 = 3
F1N, F2N, F3N = 1024, 512, 256
KD = 7
DEEP_ROWS = M * ROW + ND
LAST_E = M * ROW - (KD - 1) * P
LAST_K = LAST_E + ND
GROUPS = B // CHUNK
HP_SLOTS = 4

UNITS = ["A", 0, 1, ("K", 0), 2, ("K", 1), 3, ("K", 2), 4, 5, 6, 7, 8, 9, 10, 11, 12]
UNITS_LAST = [u for u in UNITS if isinstance(u, int)]
BY_DMA = [2, 3, 4, 6, 9, 11]
BY_POOL = [7, 10, 12]
XB_SLOTS = 3
XP_SLOTS = 2
PER_SLOT = len(BY_DMA) // XB_SLOTS
L2_LAG = 4
K_LAG = 6
PROLOGUE_UNITS = 1 + K1
POS_TURN = 13
POS_DEEP = (2, 6)
KEPT_M = 1


def pair_rows():
    rows = [(k, p) for k in range(K1) for p in range(P)]
    free = {h: [r for r in rows if r[1] % M == h] for h in range(M)}
    second = {}
    for h in range(M):
        for gap in range(M // 2 + 1):
            m = (h + gap) % M
            if gap == M // 2 and h > m:
                continue
            own, other = (h, m) if free[h] else (m, h)
            second[free[own].pop(0)] = other
    assert len(second) == M * (M + 1) // 2
    return second


def is_k(unit):
    return isinstance(unit, tuple)


def is_l2(unit):
    return isinstance(unit, int)


def is_spread(unit):
    return unit not in BY_DMA and unit not in BY_POOL


def is_multiplied(unit):
    return is_l2(unit) and unit not in BY_POOL


def count(kind, units, pos):
    return sum(kind(u) for u in units[:pos])


N_SPREADS = count(is_spread, UNITS, len(UNITS))
N_MULTIPLIED = count(is_multiplied, UNITS, len(UNITS))


def build(nc, table, sparse, dense_t, lin_dense, pair_a, pair_b, w2rows, conv1_b, conv2_b, cin_w,
          scalars, W1, b1, W2, b2, W3, b3, deep_w, sel_first, sel_second, sel_pair, ident_b, ident_f,
          out):
    with ExitStack() as ctx:
        def sb(name, shape, dt=F32):
            return ctx.enter_context(nc.sbuf_tensor(name, shape, dt))

        def pb(name, shape, dt=F32):
            return ctx.enter_context(nc.psum_tensor(name, shape, dt))

        def sem(name):
            return ctx.enter_context(nc.semaphore(name))

        deep_t = sb("deep_t", [P, KD, B])
        sum1 = sb("sum1", [H + ND, B])
        sum2 = sb("sum2", [P, B])
        lin_sum = sb("lin_sum", [P, TILES])
        idf = sb("idf", [P, P])
        wd1_kept = sb("wd1_kept", [P, KD, KEPT_M * P])
        bd1 = sb("bd1", [P, F1N // P])
        bd2 = sb("bd2", [P, F2N // P])
        bd3 = sb("bd3", [P, F3N // P])
        wdo = sb("wdo", [P, F3N // P])
        cw1 = sb("cw1", [H + ND, 1])
        cw2 = sb("cw2", [P, 1])
        sc3 = sb("sc3", [P, 3])
        bias_out = sb("bias_out", [P, 1])
        orow = sb("orow", [P, CHUNK])
        IDX_N = TILES * M

        def at_start(n, first_col, pattern, **sizes):
            return sum2[:, first_col:first_col + n].rearrange(pattern, **sizes)

        raw_idx = at_start(IDX_N, 0, "p (t m) -> p t m", m=M).bitcast(I32)
        field_base = at_start(IDX_N, IDX_N, "p (t m) -> p t m", m=M).bitcast(I32)
        wrapped = at_start(IDX_N, 2 * IDX_N, "p (t m) -> p t m", m=M)
        w1a = at_start(K1 * P, 3 * IDX_N, "p (k o) -> p k o", k=K1)
        w1b = at_start(K1 * P, 3 * IDX_N + K1 * P, "p (k o) -> p k o", k=K1)

        cin = ExitStack()

        def sc(name, shape, dt=F32):
            return cin.enter_context(nc.sbuf_tensor(name, shape, dt))

        idx_all = sc("idx_all", [P, TILES, M], I32)
        idx_stage = sc("idx_stage", [P, M], I32)
        idb = sc("idb", [P, P], BF16)
        selA = sc("selA", [PM, P], BF16)
        selK = sc("selK", [PM, K1, P], BF16)
        selJ = sc("selJ", [PM, PAIRS, P], BF16)
        w1s = sc("w1s", [P, K1, P])
        w1_hi = sc("w1_hi", [P, K1, P], F32R)
        w1_lo = sc("w1_lo", [P, K1, P], F32R)
        w2s = sc("w2s", [P, PAIRS, H])
        bias1 = sc("bias1", [P, 1])
        bias2 = sc("bias2", [P, 1])
        emb = sc("emb", [P, M, ROW])
        rem = sc("rem", [P, M, D])
        parts = sc("parts", [P, D, PM], BF16)
        x0t = [sc(f"x0t{i}", [PM, COLS], BF16) for i in range(2)]
        first = [sc(f"first{i}", [P, COLS]) for i in range(2)]
        xk = [sc(f"xk{i}", [P, COLS]) for i in range(2)]
        r1 = [sc(f"r1_{i}", [H, COLS]) for i in range(2)]
        r2 = [sc(f"r2_{i}", [P, CHUNK]) for i in range(2)]
        tmp1 = sc("tmp1", [H, P])
        tmp2 = sc("tmp2", [P, P])
        xb = [sc(f"xb{i}", [P, COLS]) for i in range(XB_SLOTS)]
        xp = [sc(f"xp{i}", [P, COLS]) for i in range(XP_SLOTS)]
        hp = [sc(f"hp{i}", [P, COLS]) for i in range(HP_SLOTS)]
        pp = [sc(f"pp{i}", [P, COLS]) for i in range(len(BY_POOL))]
        kp = sc("kp", [P, COLS])
        k_hi = [sc(f"k_hi{i}", [P, COLS], F32R) for i in range(2)]
        k_lo = [sc(f"k_lo{i}", [P, COLS], F32R) for i in range(2)]
        cin.close()
        wd1_late = sb("wd1_late", [P, KD, F1N - KEPT_M * P])
        wd2 = sb("wd2", [P, F1N // P, F2N])
        wd3 = sb("wd3", [P, F2N // P, F3N])
        h1 = sb("h1", [P, F1N // P, CHUNK])
        h2 = sb("h2", [P, F2N // P, CHUNK])
        h3 = sb("h3", [P, F3N // P, B])
        rows = nc.dram_tensor("x0_rows", (2, M, COLS), F32, kind="Internal").ap()

        bc = [pb(f"bc{i}", [P, COLS]) for i in range(2)]
        xn = pb("xn", [P, COLS])
        y2 = pb("y2", [P, CHUNK])
        tr = pb("tr", [P, CHUNK])
        tr_b = tr[:, :].bitcast(BF16)

        idx_loaded = sem("idx_loaded")
        sel_loaded = sem("sel_loaded")
        w1_loaded = sem("w1_loaded")
        w2_loaded = sem("w2_loaded")
        deep_loaded = sem("deep_loaded")
        end_loaded = sem("end_loaded")
        late_loaded = [sem(f"late_loaded{i}") for i in range(F1N // P - KEPT_M)]
        wd2_loaded = sem("wd2_loaded")
        wd3_loaded = sem("wd3_loaded")
        iota_done = sem("iota_done")
        idx_step = sem("idx_step")
        w1_step = sem("w1_step")
        bias_summed = sem("bias_summed")
        idx_staged = sem("idx_staged")
        pool_held = sem("pool_held")
        sp_held = sem("sp_held")
        gathered = sem("gathered")
        split = sem("split")
        lin_done = sem("lin_done")
        x0t_turned = sem("x0t_turned")
        x0t_copied = sem("x0t_copied")
        deep_turned = sem("deep_turned")
        deep_copied = sem("deep_copied")
        spread = sem("spread")
        first_copied = sem("first_copied")
        rows_written = sem("rows_written")
        filled = [sem(f"filled{i}") for i in range(XB_SLOTS)]
        filled_p = [sem(f"filled_p{i}") for i in range(XP_SLOTS)]
        multiplied = sem("multiplied")
        pool_multiplied = sem("pool_multiplied")
        k_made = sem("k_made")
        k_high = sem("k_high")
        k_low = sem("k_low")
        contracted = sem("contracted")
        k_contracted = sem("k_contracted")
        xn_read = sem("xn_read")
        y2_read = sem("y2_read")
        r1_reduced = sem("r1_reduced")
        r1_added = sem("r1_added")
        r2_reduced = sem("r2_reduced")
        r2_added = sem("r2_added")
        acc_ready = sem("acc_ready")
        act_done = sem("act_done")
        out_ready = sem("out_ready")
        row_ready = sem("row_ready")
        stored = sem("stored")

        def spread_by(s, pos, units=UNITS):
            return s * N_SPREADS + (PROLOGUE_UNITS + count(is_spread, units, pos + 1))

        def multiplied_by(s, pos, units=UNITS):
            return s * N_MULTIPLIED + count(is_multiplied, units, pos + 1)

        def contracted_by(s, pos, units=UNITS):
            return s * PAIRS + count(is_l2, units, pos + 1)

        def k_by(s, k):
            return s * K1 + (K1 + k + 1)

        def bc_slot(sl, units, pos):
            return (sl * N_SPREADS + count(is_spread, units, pos)) % 2

        def hp_slot(sl, units, pos):
            return (sl * N_MULTIPLIED + count(is_multiplied, units, pos)) % HP_SLOTS

        def k_slot(sl, k):
            return ((sl + 1) * K1 + k) % 2

        def filled_p_through(s, sl, slot):
            per_tile = STEPS * len(BY_POOL) // XP_SLOTS
            before = sum((n % XP_SLOTS) == slot for n in range(sl * len(BY_POOL)))
            return (s - sl) * (16 * per_tile // STEPS) + 16 * before

        def filled_p_by(s, sl, n):
            i = sl * len(BY_POOL) + n
            per_tile = STEPS * len(BY_POOL) // XP_SLOTS
            return (s - sl) * (16 * per_tile // STEPS) + 16 * (i // XP_SLOTS + 1)

        assert (16 * STEPS * len(BY_POOL) // XP_SLOTS) % STEPS == 0

        SPLITS = 4
        GATHER_RUN = -(-M // (2 * len(BY_POOL)))
        GATHERED = 16 * M

        def part(i):
            return parts[:, :, i * M:(i + 1) * M].rearrange("p d m -> p m d")

        def over_tiles(eng, tile):
            tile(0, True, False)
            with eng.Fori(1, TILES - 1) as t:
                tile(t, False, False)
            tile(TILES - 1, False, True)

        block = ctx.enter_context(nc.Block())

        SEL_LOADED, W1_LOADED, W2_LOADED, DEEP_LOADED, END_LOADED = 64, 48, 48, 112, 112
        ALL_STEPS = TILES * STEPS

        @block.sync
        def _(sp):
            sp.dma_start(raw_idx, sparse.rearrange("(t p) m -> p t m", p=P)).then_inc(idx_loaded, 16)
            for dst, src in ((idb[:, :], ident_b), (selA[:, :], sel_first),
                             (selK[:, :, :], sel_second), (selJ[:, :, :], sel_pair)):
                sp.dma_start(dst, src).then_inc(sel_loaded, 16)
            for dst, src in ((w1a, pair_a), (w1b, pair_b),
                             (bias1[:, :], conv1_b.rearrange("(p o) -> p o", o=1))):
                sp.dma_start(dst, src).then_inc(w1_loaded, 16)
            sp.dma_start(w2s[:, :, :], w2rows).then_inc(w2_loaded, 16)
            for c in range(2):
                sp.dma_start(bias2[H * c:H * c + H, :], conv2_b[H:2 * H].rearrange("(p o) -> p o", o=1)).then_inc(w2_loaded, 16)
            W1_rows = W1[0:(KD - 1) * P, :].rearrange("(k p) n -> p k n", p=P)
            W1_tail = W1[(KD - 1) * P:DEEP_ROWS, :]
            for dst, src in ((idf[:, :], ident_f),
                             (deep_t[LAST_E:LAST_K, KD - 1, :], dense_t),
                             (wd1_kept[:, 0:KD - 1, :], W1_rows[:, :, 0:KEPT_M * P]),
                             (wd1_kept[0:LAST_K, KD - 1, :], W1_tail[:, 0:KEPT_M * P]),
                             (bd1[:, :], b1), (bd2[:, :], b2), (bd3[:, :], b3)):
                sp.dma_start(dst, src).then_inc(deep_loaded, 16)
            for dst, src in ((wdo[:, :], deep_w),
                             (cw1[0:H, :], cin_w[0:H, :]), (cw2[0:H, :], cin_w[H:2 * H, :]),
                             (cw2[H:P, :], cin_w[H:2 * H, :]),
                             (cw1[H:H + ND, :], lin_dense.rearrange("(p o) -> p o", o=1)),
                             (sum1[H:H + ND, :], dense_t), (sc3[:, :], scalars)):
                sp.dma_start(dst, src).then_inc(end_loaded, 16)

            def hold():
                sp.sem_inc(sp_held, 1)

            def write_rows(s, sl):
                sp.wait_ge(first_copied, s + 1)
                hold()
                sp.dma_start(rows[sl % 2, :, :], first[sl % 2][0:M, :]).then_inc(rows_written, 16)

            def spread_rows(sl, unit):
                return rows[sl % 2, 2 * unit:2 * unit + 2, :].unsqueeze(1).to_broadcast([2, H, COLS])

            def fill(s, sl, n, units, is_first):
                if n >= XB_SLOTS:
                    sp.wait_ge(multiplied, multiplied_by(s, units.index(BY_DMA[n - XB_SLOTS]), units))
                    hold()
                elif not is_first:
                    sp.wait_ge(multiplied, multiplied_by(s - 1, UNITS.index(BY_DMA[n - XB_SLOTS])))
                    hold()
                sp.dma_start(xb[n % XB_SLOTS][:, :], spread_rows(sl, BY_DMA[n])).then_inc(filled[n % XB_SLOTS], 16)

            def fill_p(s, sl, n, is_first):
                if not is_first:
                    sp.wait_ge(pool_multiplied, s * len(BY_POOL) + (n - XP_SLOTS + 1))
                    hold()
                slot = (sl * len(BY_POOL) + n) % XP_SLOTS
                sp.dma_start(xp[slot][:, :], spread_rows(sl, BY_POOL[n])).then_inc(filled_p[slot], 16)

            write_rows(0, 0)
            sp.wait_ge(rows_written, 16)
            fill_p(0, 0, 0, True)
            fill(0, 0, 0, UNITS, True)
            fill(0, 0, 1, UNITS, True)
            fill_p(0, 0, 1, True)
            fill(0, 0, 2, UNITS, True)

            def tile(t, is_first, is_last):
                for sl in range(STEPS):
                    s = t * STEPS + sl
                    final = is_last and sl == STEPS - 1
                    units = UNITS_LAST if final else UNITS
                    fill(s, sl, 3, units, False)
                    fill_p(s, sl, 2, False)
                    fill(s, sl, 4, units, False)
                    if not final:
                        if not (is_first and sl == 0):
                            for sem_ in filled:
                                sp.wait_ge(sem_, s * (16 * PER_SLOT))
                                hold()
                            for i, sem_ in enumerate(filled_p):
                                sp.wait_ge(sem_, filled_p_through(s, sl, i))
                                hold()
                        write_rows(s + 1, sl + 1)
                    fill(s, sl, 5, units, False)
                    if not final:
                        sp.wait_ge(rows_written, s * 16 + 32)
                        hold()
                        fill_p(s + 1, sl + 1, 0, False)
                        fill(s + 1, sl + 1, 0, UNITS, False)
                        fill(s + 1, sl + 1, 1, UNITS, False)
                        fill_p(s + 1, sl + 1, 1, False)
                        fill(s + 1, sl + 1, 2, UNITS, False)

            over_tiles(sp, tile)

            sp.wait_ge(contracted, ALL_STEPS * PAIRS)
            sp.wait_ge(y2_read, ALL_STEPS)
            sp.wait_ge(r1_added, TILES * (STEPS - 1))
            sp.wait_ge(r2_added, TILES * (STEPS - 1))
            for i, loaded in enumerate(late_loaded):
                cols = slice(i * P, (i + 1) * P)
                src = slice((KEPT_M + i) * P, (KEPT_M + i + 1) * P)
                sp.dma_start(wd1_late[:, 0:KD - 1, cols], W1_rows[:, :, src]).then_inc(loaded, 16)
                sp.dma_start(wd1_late[0:LAST_K, KD - 1, cols], W1_tail[:, src]).then_inc(loaded, 16)
            sp.dma_start(wd2[:, :, :], W2.rearrange("(k p) n -> p k n", p=P)).then_inc(wd2_loaded, 16)
            sp.dma_start(wd3[:, :, :], W3.rearrange("(k p) n -> p k n", p=P)).then_inc(wd3_loaded, 16)
            sp.wait_ge(row_ready, GROUPS)
            sp.dma_start(out.rearrange("(g n) -> g n", n=CHUNK),
                         orow[0:32 * (GROUPS - 1) + 1:32, :]).then_inc(stored, 16)
            sp.wait_ge(stored, 16)

        @block.gpsimd
        def _(pool):
            nc.gpsimd.iota(field_base, [[0, TILES], [V, M]], base=0, channel_multiplier=0).then_inc(iota_done, 1)

            def hold():
                pool.sem_inc(pool_held, 1)

            def stage(t):
                hold()
                nc.gpsimd.tensor_copy(idx_stage[:, :], idx_all[:, bass.ds(t, 1), :].rearrange("p a m -> p (a m)")).then_inc(idx_staged, 1)
                pool.wait_ge(idx_staged, t + 1)
                hold()

            def gather(fields):
                for m in fields:
                    nc.gpsimd.indirect_dma_start(
                        out=emb[:, m, :], out_offset=None, in_=table,
                        in_offset=bass.IndirectOffsetOnAxis(ap=idx_stage[:, m:m + 1], axis=0)).then_inc(gathered, 16)

            def split_parts(t):
                pool.wait_ge(gathered, t * GATHERED + GATHERED)
                hold()
                nc.gpsimd.tensor_copy(part(0), emb[:, :, 0:D]).then_inc(split, 1)
                pool.wait_ge(split, t * SPLITS + 1)
                nc.gpsimd.tensor_tensor(rem[:, :, :], emb[:, :, 0:D], part(0), ALU.subtract).then_inc(split, 1)
                pool.wait_ge(split, t * SPLITS + 2)
                hold()
                nc.gpsimd.tensor_copy(part(1), rem[:, :, :]).then_inc(split, 1)
                pool.wait_ge(split, t * SPLITS + 3)
                nc.gpsimd.tensor_tensor(part(2), rem[:, :, :], part(1), ALU.subtract).then_inc(split, 1)

            def multiply(t, sl, n, is_start):
                s = t * STEPS + sl
                slot = (sl * len(BY_POOL) + n) % XP_SLOTS
                if n == 0:
                    pool.wait_ge(xn_read, s + 1)
                pool.wait_ge(filled_p[slot], filled_p_by(s, sl, n))
                if not is_start:
                    pool.wait_ge(contracted, contracted_by(s - 1, UNITS.index(BY_POOL[n])))
                nc.gpsimd.tensor_tensor(pp[n][:, :], xp[slot][:, :], xk[sl % 2][:, :], ALU.mult).then_inc(pool_multiplied, 1)

            pool.wait_ge(idx_step, 4)
            stage(0)
            gather(range(M))

            def tile(t, is_first, is_last):
                if not is_last:
                    pool.wait_ge(split, t * SPLITS + SPLITS)
                    pool.wait_ge(deep_turned, t * 2 + 2)
                    pool.wait_ge(lin_done, t + 1)
                    stage(t + 1)
                for n in range(2 * len(BY_POOL)):
                    if not is_last:
                        gather(range(n * GATHER_RUN, min(M, (n + 1) * GATHER_RUN)))
                    multiply(t, n // len(BY_POOL), n % len(BY_POOL), is_first and n < len(BY_POOL))
                if not is_last:
                    pool.wait_ge(x0t_turned, t * STEPS + STEPS)
                    split_parts(t + 1)
                for sl in (2, 3):
                    for n in range(len(BY_POOL)):
                        multiply(t, sl, n, False)

            over_tiles(pool, tile)

        @block.vector
        def _(dve):
            dve.wait_ge(idx_loaded, 16)
            nc.vector.tensor_scalar(wrapped, raw_idx, 0.0, float(V), ALU.is_lt, ALU.mult).then_inc(idx_step, 1)
            dve.wait_ge(idx_step, 1)
            nc.vector.tensor_tensor(wrapped, wrapped, raw_idx, ALU.add).then_inc(idx_step, 1)
            dve.wait_ge(idx_step, 2)
            nc.vector.tensor_scalar(wrapped, wrapped, 0.0, float(V - 1), ALU.max, ALU.min).then_inc(idx_step, 1)
            dve.wait_ge(idx_step, 3)
            dve.wait_ge(iota_done, 1)
            nc.vector.tensor_tensor(idx_all[:, :, :], wrapped, field_base, ALU.add).then_inc(idx_step, 1)
            dve.wait_ge(w1_loaded, W1_LOADED)
            nc.vector.tensor_tensor(w1s[:, :, :], w1a, w1b, ALU.add).then_inc(w1_step, 1)
            dve.wait_ge(w1_step, 1)
            nc.vector.tensor_copy(w1_hi[:, :, :], w1s[:, :, :]).then_inc(w1_step, 1)
            dve.wait_ge(w1_step, 2)
            nc.vector.tensor_tensor(w1_lo[:, :, :], w1s[:, :, :], w1_hi[:, :, :], ALU.subtract).then_inc(w1_step, 1)
            dve.wait_ge(end_loaded, END_LOADED)
            nc.vector.tensor_reduce(bias_out[:, :], sc3[:, :], AX_X, ALU.add).then_inc(bias_summed, 1)
            dve.wait_ge(gathered, GATHERED)
            nc.vector.tensor_copy(part(0), emb[:, :, 0:D]).then_inc(split, 1)
            dve.wait_ge(split, 1)
            nc.vector.tensor_tensor(rem[:, :, :], emb[:, :, 0:D], part(0), ALU.subtract).then_inc(split, 1)
            dve.wait_ge(split, 2)
            nc.vector.tensor_copy(part(1), rem[:, :, :]).then_inc(split, 1)
            dve.wait_ge(split, 3)
            nc.vector.tensor_tensor(part(2), rem[:, :, :], part(1), ALU.subtract).then_inc(split, 1)

            def sum_linear(t):
                dve.wait_ge(gathered, t * GATHERED + GATHERED)
                nc.vector.tensor_reduce(lin_sum[:, bass.ds(t, 1)], emb[:, :, D], AX_X, ALU.add).then_inc(lin_done, 1)

            sum_linear(0)

            def k_product(s, sl, k, spread_count, slot, is_first):
                if k == 0:
                    dve.wait_ge(first_copied, s + 2)
                dve.wait_ge(spread, spread_count)
                if not is_first:
                    dve.wait_ge(k_low, k_by(s, k) - 1)
                nc.vector.tensor_tensor(kp[:, :], bc[slot][:, :], first[(sl + 1) % 2][:, :], ALU.mult).then_inc(k_made, 1)

            def k_lower(s, sl, k, is_early):
                slot = k_slot(sl, k)
                dve.wait_ge(k_high, k_by(s, k))
                if not is_early:
                    dve.wait_ge(k_contracted, k_by(s, k) - 2)
                nc.vector.tensor_tensor(k_lo[slot][:, :], kp[:, :], k_hi[slot][:, :], ALU.subtract).then_inc(k_low, 1)

            for k in range(K1):
                k_product(-1, -1, k, 2 + k, (1 + k) % 2, k == 0)
                k_lower(-1, -1, k, k < 2)

            def reduce_r1(t, sl):
                s = t * STEPS + sl
                dve.wait_ge(xn_read, s + 1)
                if sl > 0:
                    if sl > 1 or not isinstance(t, int) or t > 0:
                        dve.wait_ge(r1_added, t * (STEPS - 1) + (sl - 1))
                    dst = tmp1[:, :]
                else:
                    dst = sum1[0:H, bass.ds(t * P, P)]
                nc.vector.tensor_reduce(dst, r1[sl % 2][:, :].rearrange("p (q b) -> p b q", b=P), AX_X, ALU.add).then_inc(r1_reduced, 1)

            def add_r1(t, sl):
                dve.wait_ge(r1_reduced, t * STEPS + (sl + 1))
                acc = sum1[0:H, bass.ds(t * P, P)]
                nc.vector.tensor_tensor(acc, acc, tmp1[:, :], ALU.add).then_inc(r1_added, 1)

            def reduce_r2(t, sl):
                s = t * STEPS + sl
                dve.wait_ge(y2_read, s + 1)
                if sl > 0:
                    if sl > 1 or not isinstance(t, int) or t > 0:
                        dve.wait_ge(r2_added, t * (STEPS - 1) + (sl - 1))
                    dst = tmp2[:, :]
                else:
                    dst = sum2[:, bass.ds(t * P, P)]
                nc.vector.tensor_reduce(dst, r2[sl % 2][:, :].rearrange("p (q b) -> p b q", b=P), AX_X, ALU.add).then_inc(r2_reduced, 1)

            def add_r2(t, sl):
                dve.wait_ge(r2_reduced, t * STEPS + (sl + 1))
                acc = sum2[:, bass.ds(t * P, P)]
                nc.vector.tensor_tensor(acc, acc, tmp2[:, :], ALU.add).then_inc(r2_added, 1)

            def tile(t, is_first, is_last):
                for sl in range(STEPS):
                    s = t * STEPS + sl
                    start = is_first and sl == 0
                    units = UNITS_LAST if is_last and sl == STEPS - 1 else UNITS
                    before = (t, sl - 1) if sl else (t - 1, STEPS - 1)
                    k_waiting = None
                    for pos, unit in enumerate(units):
                        if is_k(unit):
                            k_product(s, sl, unit[1], spread_by(s, pos), bc_slot(sl, units, pos), False)
                            k_waiting = unit[1]
                        elif is_multiplied(unit):
                            if unit == 0:
                                dve.wait_ge(xn_read, s + 1)
                            if is_spread(unit):
                                dve.wait_ge(spread, spread_by(s, pos, units))
                                x = bc[bc_slot(sl, units, pos)]
                            else:
                                n = BY_DMA.index(unit)
                                x = xb[n % XB_SLOTS]
                                dve.wait_ge(filled[n % XB_SLOTS], s * (16 * PER_SLOT) + 16 * (n // XB_SLOTS + 1))
                            mine = [u for u in units if is_multiplied(u)]
                            at = mine.index(unit)
                            if at >= HP_SLOTS:
                                dve.wait_ge(contracted, contracted_by(s, units.index(mine[at - HP_SLOTS]), units))
                            elif not start:
                                dve.wait_ge(contracted, contracted_by(s - 1, UNITS.index(mine[at - HP_SLOTS])))
                            nc.vector.tensor_tensor(hp[hp_slot(sl, units, pos)][:, :], x[:, :], xk[sl % 2][:, :], ALU.mult).then_inc(multiplied, 1)
                            if k_waiting is not None:
                                k_lower(s, sl, k_waiting, False)
                                k_waiting = None
                        if unit == 1:
                            reduce_r1(t, sl)
                        if unit == 4 and sl:
                            add_r1(t, sl)
                        if unit == 6 and not start:
                            reduce_r2(*before)
                        if unit == 8 and not start and before[1]:
                            add_r2(*before)
                        if unit == 5 and sl == STEPS - 1 and not is_last:
                            sum_linear(t + 1)

            over_tiles(dve, tile)
            reduce_r2(TILES - 1, STEPS - 1)
            add_r2(TILES - 1, STEPS - 1)

        N_ACC = (F1N + F2N + F3N) // P

        @block.tensor
        def _(pe):
            def turn_x0(sl):
                for q in range(STEP_D):
                    last = nc.tensor.transpose(tr_b[0:PM, q * P:(q + 1) * P], parts[:, sl * STEP_D + q, :], idb[:, :])
                last.then_inc(x0t_turned, 1)

            def turn_deep(half):
                numbers = emb[:, :, :].rearrange("p m e -> p (m e)")
                for i, k in enumerate((range(4), range(4, KD))[half]):
                    n = min(P, M * ROW - k * P)
                    last = nc.tensor.transpose(tr[0:n, i * P:(i + 1) * P], numbers[:, k * P:k * P + n], idf[:, :])
                last.then_inc(deep_turned, 1)

            def broadcast(unit, slot, sl):
                x = x0t[sl % 2] if is_l2(unit) else x0t[(sl + 1) % 2]
                sel = selJ[:, unit, :] if is_l2(unit) else selA[:, :] if unit == "A" else selK[:, unit[1], :]
                for c in range(2):
                    last = nc.tensor.matmul(bc[slot][:, c * CHUNK:(c + 1) * CHUNK], sel, x[:, c * CHUNK:(c + 1) * CHUNK],
                                            start=True, stop=True)
                last.then_inc(spread, 1)

            def contract_k(s, sl, k, is_first):
                if k == 0 and not is_first:
                    pe.wait_ge(xn_read, s + 1)
                pe.wait_ge(k_high, k_by(s, k))
                pe.wait_ge(k_low, k_by(s, k))
                slot = k_slot(sl, k)
                for i, (w, x) in enumerate(((w1_hi, k_hi), (w1_lo, k_hi), (w1_hi, k_lo))):
                    for c in range(2):
                        cols = slice(c * CHUNK, (c + 1) * CHUNK)
                        last = nc.tensor.matmul(xn[:, cols], w[:, k, :], x[slot][:, cols],
                                                start=(k == 0 and i == 0), stop=(k == K1 - 1 and i == 2))
                last.then_inc(k_contracted, 1)

            def contract(s, sl, pos, units, is_start):
                unit = units[pos]
                if unit == 0 and not is_start:
                    pe.wait_ge(y2_read, s)
                if unit in BY_POOL:
                    n = BY_POOL.index(unit)
                    pe.wait_ge(pool_multiplied, s * len(BY_POOL) + (n + 1))
                    src = pp[n]
                else:
                    pe.wait_ge(multiplied, multiplied_by(s, pos, units))
                    src = hp[hp_slot(sl, units, pos)]
                for c in range(2):
                    last = nc.tensor.matmul(y2[H * c:H * c + H, :], w2s[:, unit, :], src[:, c * CHUNK:(c + 1) * CHUNK],
                                            start=(unit == 0), stop=(unit == PAIRS - 1))
                last.then_inc(contracted, 1)

            pe.wait_ge(sel_loaded, SEL_LOADED)
            pe.wait_ge(split, SPLITS)
            turn_x0(0)
            pe.wait_ge(x0t_copied, 1)
            broadcast("A", 0, -1)
            broadcast(("K", 0), 1, -1)
            turn_x0(1)
            pe.wait_ge(first_copied, 1)
            broadcast(("K", 1), 0, -1)
            pe.wait_ge(k_made, 1)
            broadcast(("K", 2), 1, -1)
            pe.wait_ge(w1_step, 3)
            for k in range(K1):
                contract_k(-1, -1, k, True)
            pe.wait_ge(deep_loaded, DEEP_LOADED)
            pe.wait_ge(x0t_copied, 2)
            turn_deep(0)
            pe.wait_ge(deep_copied, 1)
            turn_deep(1)
            pe.wait_ge(w2_loaded, W2_LOADED)

            def tile(t, is_first, is_last):
                for sl in range(STEPS):
                    s = t * STEPS + sl
                    start = is_first and sl == 0
                    final = is_last and sl == STEPS - 1
                    units = UNITS_LAST if final else UNITS
                    for pos, unit in enumerate(units):
                        if pos == 0:
                            pe.wait_ge(x0t_copied, s + (1 if final else 2))
                        if is_spread(unit):
                            mine = [q for q in range(len(units)) if is_spread(units[q])]
                            at = mine.index(pos)
                            q = mine[at - 2] if at >= 2 else [q for q in range(len(UNITS)) if is_spread(UNITS[q])][at - 2]
                            of, us, ss = (UNITS[q], UNITS, s - 1) if at < 2 else (units[q], units, s)
                            if at < 2 and start:
                                pe.wait_ge(k_made, K1 - 1 + at)
                            elif of == "A":
                                pe.wait_ge(first_copied, ss + 2)
                            elif is_k(of):
                                pe.wait_ge(k_made, k_by(ss, of[1]))
                            else:
                                pe.wait_ge(multiplied, multiplied_by(ss, q, us))
                            broadcast(unit, bc_slot(sl, units, pos), sl)
                        if sl == STEPS - 1 and not is_last and pos in POS_DEEP:
                            half = POS_DEEP.index(pos)
                            if half:
                                pe.wait_ge(deep_copied, t * 2 + 3)
                            turn_deep(half)
                        if pos == POS_TURN and not (is_last and sl >= 2):
                            if sl == STEPS - 1 or (is_first and sl == 0):
                                pe.wait_ge(deep_copied, t * 2 + (4 if sl else 2))
                            if sl == 2:
                                pe.wait_ge(split, t * SPLITS + 2 * SPLITS)
                            turn_x0((sl + 2) % STEPS)
                        if pos >= K_LAG and is_k(units[pos - K_LAG]):
                            contract_k(s, sl, units[pos - K_LAG][1], False)
                        if pos >= L2_LAG and is_l2(units[pos - L2_LAG]):
                            contract(s, sl, pos - L2_LAG, units, start)
                        elif pos < L2_LAG and not start:
                            contract(s - 1, sl - 1, len(UNITS) - L2_LAG + pos, UNITS, False)
                if is_last:
                    for pos in range(PAIRS - L2_LAG, PAIRS):
                        contract(ALL_STEPS - 1, STEPS - 1, pos, UNITS_LAST, False)

            over_tiles(pe, tile)

            def deep_group(g, is_first):
                cols = bass.ds(g * CHUNK, CHUNK)
                base = g * N_ACC

                def layer(at, tiles, weights, rows, rhs, inputs, loaded):
                    for m in range(tiles):
                        if is_first and loaded(m) is not None:
                            pe.wait_ge(*loaded(m))
                        a = at + m
                        if not (is_first and a < 2):
                            pe.wait_ge(act_done, base + (a - 1))
                        for k in range(rows):
                            if m == 0 and inputs is not None:
                                pe.wait_ge(act_done, base + (inputs + k + 1))
                            kp = LAST_K if inputs is None and k == rows - 1 else P
                            last = nc.tensor.matmul(bc[a % 2][:, 0:CHUNK], weights(m, k, kp),
                                                    rhs(k, kp), start=(k == 0), stop=(k == rows - 1))
                        last.then_inc(acc_ready, 1)

                def first_weights(m, k, kp):
                    kept = m < KEPT_M
                    w, at = (wd1_kept, m) if kept else (wd1_late, m - KEPT_M)
                    return w[0:kp, k, at * P:(at + 1) * P]

                layer(0, F1N // P, first_weights, KD, lambda k, kp: deep_t[0:kp, k, cols], None,
                      lambda m: None if m < KEPT_M else (late_loaded[m - KEPT_M], 32))
                layer(F1N // P, F2N // P, lambda m, k, kp: wd2[:, k, m * P:(m + 1) * P], F1N // P,
                      lambda k, kp: h1[:, k, :], 0, lambda m: None if m else (wd2_loaded, 16))
                layer((F1N + F2N) // P, F3N // P, lambda m, k, kp: wd3[:, k, m * P:(m + 1) * P], F2N // P,
                      lambda k, kp: h2[:, k, :], F1N // P, lambda m: None if m else (wd3_loaded, 16))

            pe.wait_ge(multiplied, ALL_STEPS * N_MULTIPLIED)
            pe.wait_ge(deep_copied, 2 * TILES)
            deep_group(0, True)
            with pe.Fori(1, GROUPS) as g:
                deep_group(g, False)

            pe.wait_ge(end_loaded, END_LOADED)
            pe.wait_ge(xn_read, ALL_STEPS)
            pe.wait_ge(r1_reduced, ALL_STEPS)
            pe.wait_ge(r1_added, TILES * (STEPS - 1))
            pe.wait_ge(r2_added, TILES * (STEPS - 1))
            pe.wait_ge(lin_done, TILES)
            terms = [(cw1[:, :], sum1[:, :]), (cw2[:, :], sum2[:, :])]
            terms += [(wdo[:, k:k + 1], h3[:, k, :]) for k in range(F3N // P)]
            for n, (w, x) in enumerate(terms):
                if n == 2:
                    pe.wait_ge(act_done, GROUPS * N_ACC)
                for g in range(GROUPS):
                    nc.tensor.matmul(xn[32 * g:32 * g + 1, 0:CHUNK], w, x[:, g * CHUNK:(g + 1) * CHUNK],
                                     start=(n == 0), stop=False, skip_group_check=True)
            for c in range(CHUNK // P):
                for g in range(GROUPS):
                    t = g * (CHUNK // P) + c
                    last = nc.tensor.matmul(xn[32 * g:32 * g + 1, c * P:(c + 1) * P], lin_sum[:, t:t + 1], idf[:, :],
                                            start=False, stop=True, skip_group_check=True)
            last.then_inc(out_ready, 1)

        @block.scalar
        def _(act):
            act.wait_ge(w1_loaded, W1_LOADED)

            def copy_x0(s, sl):
                act.wait_ge(x0t_turned, s + 1)
                nc.scalar.activation(x0t[sl % 2][:, :], tr_b[0:PM, :], ACT.Copy).then_inc(x0t_copied, 1)

            def copy_deep(t, half):
                act.wait_ge(deep_turned, t * 2 + (half + 1))
                cols = bass.ds(t * P, P)
                if half == 0:
                    nc.scalar.activation(deep_t[:, 0:4, cols], tr[:, :].rearrange("p (k b) -> p k b", b=P),
                                         ACT.Copy).then_inc(deep_copied, 1)
                else:
                    nc.scalar.activation(deep_t[:, 4:6, cols], tr[:, 0:2 * P].rearrange("p (k b) -> p k b", b=P), ACT.Copy)
                    nc.scalar.activation(deep_t[0:LAST_E, 6, cols], tr[0:LAST_E, 2 * P:3 * P],
                                         ACT.Copy).then_inc(deep_copied, 1)

            def upper(s, sl, k, is_early):
                slot = k_slot(sl, k)
                act.wait_ge(k_made, k_by(s, k))
                if not is_early:
                    act.wait_ge(k_contracted, k_by(s, k) - 2)
                nc.scalar.activation(k_hi[slot][:, :], kp[:, :], ACT.Copy).then_inc(k_high, 1)

            def read_xn(slot):
                nc.scalar.activation(xk[slot][0:H, :], xn[0:H, :], ACT.Sigmoid, bias=bias1[0:H, :])
                nc.scalar.activation(xk[slot][H:P, :], xn[0:H, :], ACT.Sigmoid, bias=bias1[0:H, :])
                nc.scalar.activation(r1[slot][:, :], xn[H:P, :], ACT.Sigmoid, bias=bias1[H:P, :]).then_inc(xn_read, 1)

            def read_y2(s, slot, is_early):
                act.wait_ge(contracted, s * PAIRS + PAIRS)
                if not is_early:
                    act.wait_ge(r2_reduced, s - 1)
                nc.scalar.activation(r2[slot][:, :], y2[:, :], ACT.Sigmoid, bias=bias2[:, :]).then_inc(y2_read, 1)

            copy_x0(0, 0)
            act.wait_ge(spread, 1)
            nc.scalar.activation(first[0][:, :], bc[0][:, :], ACT.Copy).then_inc(first_copied, 1)
            copy_x0(1, 1)
            for k in range(K1):
                upper(-1, -1, k, k < 2)
            act.wait_ge(k_contracted, K1)
            read_xn(0)
            copy_deep(0, 0)
            copy_deep(0, 1)
            act.wait_ge(w2_loaded, W2_LOADED)

            def tile(t, is_first, is_last):
                for sl in range(STEPS):
                    s = t * STEPS + sl
                    start = is_first and sl == 0
                    final = is_last and sl == STEPS - 1
                    if not final:
                        pos = UNITS.index("A")
                        act.wait_ge(spread, spread_by(s, pos))
                        if not start:
                            act.wait_ge(k_made, s * K1)
                            act.wait_ge(rows_written, s * 16)
                        nc.scalar.activation(first[(sl + 1) % 2][:, :], bc[bc_slot(sl, UNITS, pos)][:, :],
                                             ACT.Copy).then_inc(first_copied, 1)
                    if not start:
                        read_y2(s - 1, (sl + 1) % 2, is_first and sl <= 2)
                    if final:
                        continue
                    deep = sl == STEPS - 1
                    if deep:
                        copy_deep(t + 1, 0)
                    upper(s, sl, 0, False)
                    if deep:
                        copy_deep(t + 1, 1)
                    upper(s, sl, 1, False)
                    upper(s, sl, 2, False)
                    act.wait_ge(k_contracted, k_by(s, K1 - 1))
                    if not start:
                        act.wait_ge(multiplied, s * N_MULTIPLIED)
                        act.wait_ge(pool_multiplied, s * len(BY_POOL))
                        act.wait_ge(r1_reduced, s)
                    read_xn((sl + 1) % 2)
                    if not (is_last and sl >= 2):
                        act.wait_ge(spread, s * N_SPREADS + (PROLOGUE_UNITS + N_SPREADS))
                        copy_x0(s + 2, sl + 2)

            over_tiles(act, tile)
            read_y2(ALL_STEPS - 1, (ALL_STEPS - 1) % 2, False)

            def deep_group(g):
                base = g * N_ACC
                a = 0
                for tiles, bias, dst in ((F1N // P, bd1, h1), (F2N // P, bd2, h2), (F3N // P, bd3, None)):
                    for m in range(tiles):
                        act.wait_ge(acc_ready, base + (a + 1))
                        to = dst[:, m, :] if dst is not None else h3[:, m, bass.ds(g * CHUNK, CHUNK)]
                        nc.scalar.activation(to, bc[a % 2][:, 0:CHUNK], ACT.Tanh, bias=bias[:, m:m + 1]).then_inc(act_done, 1)
                        a += 1

            act.wait_ge(deep_loaded, DEEP_LOADED)
            act.wait_ge(r1_added, TILES * (STEPS - 1))
            act.wait_ge(r2_added, TILES * (STEPS - 1))
            with act.Fori(0, GROUPS) as g:
                deep_group(g)
            act.wait_ge(bias_summed, 1)
            act.wait_ge(out_ready, 1)
            for g in range(GROUPS):
                r = slice(32 * g, 32 * g + 1)
                nc.scalar.activation(orow[r, :], xn[r, 0:CHUNK], ACT.Identity, bias=bias_out[r, :]).then_inc(row_ready, 1)


def kernel(r_dense, r_sparse, L0_rec_tables, L0_rec_lin_sparse_w, L0_rec_lin_dense_w, L0_rec_conv1_w,
           L0_rec_conv1_b, L0_rec_conv2_w, L0_rec_conv2_b, L0_rec_cin_w, L0_rec_cin_b, L0_rec_W1, L0_rec_b1,
           L0_rec_W2, L0_rec_b2, L0_rec_W3, L0_rec_b3, L0_rec_deep_w, L0_rec_deep_b, L0_rec_bias):
    import concourse.bacc as _bacc
    from concourse import mybir as _mybir
    from concourse.bass_utils import run_bass_kernel_spmd as _run

    f = np.asarray
    table = np.concatenate([f(L0_rec_tables).reshape(M * V, D), f(L0_rec_lin_sparse_w).reshape(M * V, 1)], axis=1)
    w1t = np.concatenate([f(L0_rec_conv1_w).T, np.zeros((1, P), np.float32)])
    row_a = np.full((P, K1), M * M)
    row_b = np.full((P, K1), M * M)
    second = pair_rows()
    for (k, p), m in second.items():
        h = p % M
        row_a[p, k] = h * M + m
        if m != h:
            row_b[p, k] = m * M + h
    w2 = f(L0_rec_conv2_w)[H:].reshape(H, H, PAIRS, 2).transpose(3, 1, 2, 0).reshape(P, PAIRS, H)
    deep1 = np.zeros((DEEP_ROWS, F1N), np.float32)
    deep1[:M * ROW].reshape(M, ROW, F1N)[:, :D] = f(L0_rec_W1)[:M * D].reshape(M, D, F1N)
    deep1[M * ROW:] = f(L0_rec_W1)[M * D:]
    bf = _mybir.dt.np(_mybir.dt.bfloat16)
    sel_first = np.zeros((PARTS, M, P), bf)
    sel_second = np.zeros((PARTS, M, K1, P), bf)
    sel_pair = np.zeros((PARTS, M, PAIRS, P), bf)
    for p in range(P):
        sel_first[:, p % M, p] = 1
        for j in range(PAIRS):
            sel_pair[:, 2 * j + p // H, j, p] = 1
    for (k, p), m in second.items():
        sel_second[:, m, k, p] = 1

    ins = {
        "table": table, "sparse": f(r_sparse), "dense_t": f(r_dense).T, "lin_dense": f(L0_rec_lin_dense_w),
        "pair_a": w1t[row_a], "pair_b": w1t[row_b], "w2rows": w2, "conv1_b": f(L0_rec_conv1_b),
        "conv2_b": f(L0_rec_conv2_b), "cin_w": f(L0_rec_cin_w),
        "scalars": np.tile(np.concatenate([f(L0_rec_cin_b), f(L0_rec_deep_b), f(L0_rec_bias)]), (P, 1)),
        "W1": deep1, "b1": f(L0_rec_b1).reshape(-1, P).T, "W2": f(L0_rec_W2), "b2": f(L0_rec_b2).reshape(-1, P).T, "W3": f(L0_rec_W3),
        "b3": f(L0_rec_b3).reshape(-1, P).T, "deep_w": f(L0_rec_deep_w).reshape(-1, P).T,
        "sel_first": sel_first.reshape(PM, P), "sel_second": sel_second.reshape(PM, K1, P),
        "sel_pair": sel_pair.reshape(PM, PAIRS, P),
        "ident_b": np.eye(P, dtype=bf), "ident_f": np.eye(P, dtype=np.float32),
    }
    nc = _bacc.Bacc("TRN2", target_bir_lowering=False, num_devices=1)
    arrays, args = {}, []
    for name, a in ins.items():
        a = np.ascontiguousarray(a)
        arrays[name] = a
        args.append(nc.dram_tensor(name, a.shape, _mybir.dt.from_np(a.dtype), kind="ExternalInput").ap())
    args.append(nc.dram_tensor("result", (B,), _mybir.dt.float32, kind="ExternalOutput").ap())
    build(nc, *args)
    r = _run(nc, [arrays], core_ids=[0])
    return r.results[0]["result"]
```

```python
from contextlib import ExitStack

import numpy as np

import concourse.bass as bass
from concourse import mybir

F32 = mybir.dt.float32
BF16 = mybir.dt.bfloat16
F32R = mybir.dt.float32r
I32 = mybir.dt.int32
ALU = mybir.AluOpType
ACT = mybir.ActivationFunctionType
AX_X = mybir.AxisListType.X

P = 128
B, M, V, D, ND = 2048, 26, 1250, 32, 13
ROW = D + 1
TILES = B // P
STEP_D = 8
STEPS = D // STEP_D
COLS = STEP_D * P
CHUNK = 512
H = 64
PARTS = 3
PM = PARTS * M
PAIRS = M // 2
K1 = 3
F1N, F2N, F3N = 1024, 512, 256
KD = 7
DEEP_ROWS = M * ROW + ND
LAST_E = M * ROW - (KD - 1) * P
LAST_K = LAST_E + ND
GROUPS = B // CHUNK
ACCS = [(0, m) for m in range(F1N // P)] + [(1, m) for m in range(F2N // P)] + [(2, m) for m in range(F3N // P)]
LAYER_ROWS = (KD, F1N // P, F2N // P)
HIDDEN = (F1N + F2N) // P
assert len(ACCS) % 2 == 0
HP_SLOTS = 4
K_SPLIT = 1

UNITS = ["A", ("K", 0), 0, 1, 2, ("K", 1), 3, 4, ("K", 2), 5, 6, 7, 8, 9, 10, 11, 12]
UNITS_LAST = [u for u in UNITS if isinstance(u, int)]
BY_DMA = [2, 3, 4, 6, 10, 11]
BY_POOL = [7, 12]
XB_SLOTS = 3
XP_SLOTS = 2
L2_LAG = 5
K_LAG = 6
PROLOGUE_UNITS = 1 + K1
POS_TURN = 13
POS_DEEP = (7, 10)


def pair_rows():
    rows = [(k, p) for k in range(K1) for p in range(P)]
    free = {h: [r for r in rows if r[1] % M == h] for h in range(M)}
    second = {}
    for h in range(M):
        for gap in range(M // 2 + 1):
            m = (h + gap) % M
            if gap == M // 2 and h > m:
                continue
            own, other = (h, m) if free[h] else (m, h)
            second[free[own].pop(0)] = other
    assert len(second) == M * (M + 1) // 2
    return second


def is_k(unit):
    return isinstance(unit, tuple)


def is_l2(unit):
    return isinstance(unit, int)


def is_spread(unit):
    return unit not in BY_DMA and unit not in BY_POOL


def is_multiplied(unit):
    return is_l2(unit) and unit not in BY_POOL


def count(kind, units, pos):
    return sum(kind(u) for u in units[:pos])


N_SPREADS = count(is_spread, UNITS, len(UNITS))
N_MULTIPLIED = count(is_multiplied, UNITS, len(UNITS))


def build(nc, table, sparse, dense_t, lin_dense, pair_a, pair_b, w2rows, conv1_b, conv2_b, cin_w,
          scalars, W1, b1, W2, b2, W3, b3, deep_w, sel_first, sel_second, sel_pair, ident_b, ident_f,
          out):
    with ExitStack() as ctx:
        def sb(name, shape, dt=F32):
            return ctx.enter_context(nc.sbuf_tensor(name, shape, dt))

        def pb(name, shape, dt=F32):
            return ctx.enter_context(nc.psum_tensor(name, shape, dt))

        def sem(name):
            return ctx.enter_context(nc.semaphore(name))

        deep_t = sb("deep_t", [P, KD, B])
        sum1 = sb("sum1", [P, B])
        sum2 = sb("sum2", [P, B])
        lin_sum = sb("lin_sum", [P, TILES])
        idf = sb("idf", [P, P])
        w_raw = [sb("w_raw0", [P, F1N // P, P])]
        bd1 = sb("bd1", [P, F1N // P])
        bd2 = sb("bd2", [P, F2N // P])
        bd3 = sb("bd3", [P, F3N // P])
        wdo = sb("wdo", [P, F3N // P])
        cw1 = sb("cw1", [P, 1])
        cwd = sb("cwd", [LAST_K, 1])
        cw2 = sb("cw2", [P, 1])
        sc3 = sb("sc3", [P, 3])
        bias_out = sb("bias_out", [P, 1])
        orow = sb("orow", [P, CHUNK])
        IDX_N = TILES * M

        def at_start(n, first_col, pattern, **sizes):
            return sum2[:, first_col:first_col + n].rearrange(pattern, **sizes)

        raw_idx = at_start(IDX_N, 0, "p (t m) -> p t m", m=M).bitcast(I32)
        field_base = at_start(IDX_N, IDX_N, "p (t m) -> p t m", m=M).bitcast(I32)
        wrapped = at_start(IDX_N, 2 * IDX_N, "p (t m) -> p t m", m=M)
        w1a = at_start(K1 * P, 3 * IDX_N, "p (k o) -> p k o", k=K1)
        w1b = at_start(K1 * P, 3 * IDX_N + K1 * P, "p (k o) -> p k o", k=K1)

        cin = ExitStack()

        def sc(name, shape, dt=F32):
            return cin.enter_context(nc.sbuf_tensor(name, shape, dt))

        idx_all = sc("idx_all", [P, TILES, M], I32)
        idx_stage = sc("idx_stage", [P, M], I32)
        emb = sc("emb", [P, M, ROW])
        rem = sc("rem", [P, M, D])
        parts = sc("parts", [P, D, PM], BF16)
        first = [sc(f"first{i}", [P, COLS]) for i in range(2)]
        kp = [sc(f"kp{k}", [P, COLS]) for k in range(K1)]
        k_hi = [sc(f"k_hi{i}", [P, COLS], F32R) for i in range(K_SPLIT)]
        k_lo = [sc(f"k_lo{i}", [P, COLS], F32R) for i in range(K_SPLIT)]
        idb = sc("idb", [P, P], BF16)
        selA = sc("selA", [PM, P], BF16)
        selK = sc("selK", [PM, K1, P], BF16)
        selJ = sc("selJ", [PM, PAIRS, P], BF16)
        w1s = sc("w1s", [P, K1, P])
        w1_hi = sc("w1_hi", [P, K_SPLIT, P], F32R)
        w1_lo = sc("w1_lo", [P, K_SPLIT, P], F32R)
        w2s = sc("w2s", [P, PAIRS, H])
        bias1 = sc("bias1", [P, 1])
        bias2 = sc("bias2", [P, 1])
        xb = [sc(f"xb{i}", [P, COLS]) for i in range(XB_SLOTS)]
        xp = [sc(f"xp{i}", [P, COLS]) for i in range(XP_SLOTS)]
        pp = [sc(f"pp{i}", [P, COLS]) for i in range(len(BY_POOL))]
        hp = [sc(f"hp{i}", [P, COLS]) for i in range(HP_SLOTS)]
        x0t = [sc(f"x0t{i}", [PM, COLS], BF16) for i in range(2)]
        xk = [sc(f"xk{i}", [P, COLS]) for i in range(2)]
        r1 = [sc(f"r1_{i}", [P, CHUNK]) for i in range(2)]
        r2 = [sc(f"r2_{i}", [P, CHUNK]) for i in range(2)]
        tmp1 = sc("tmp1", [P, P])
        tmp2 = sc("tmp2", [P, P])
        cin.close()
        x_hi = sb("x_hi", [P, KD, CHUNK], F32R)
        x_lo = sb("x_lo", [P, KD, CHUNK], F32R)
        w_raw.append(sb("w_raw1", [P, F1N // P, P]))
        w_hi = [sb(f"w_hi{i}", [P, F1N // P, P], F32R) for i in range(2)]
        w_lo = [sb(f"w_lo{i}", [P, F1N // P, P], F32R) for i in range(2)]
        h_raw = [sb(f"h_raw{i}", [P, CHUNK]) for i in range(2)]
        h_hi = sb("h_hi", [P, HIDDEN, CHUNK], F32R)
        h_lo = sb("h_lo", [P, HIDDEN, CHUNK], F32R)
        h3 = sb("h3", [P, F3N // P, B])
        rows = nc.dram_tensor("x0_rows", (2, M, COLS), F32, kind="Internal").ap()

        bc = [pb(f"bc{i}", [P, COLS]) for i in range(2)]
        xn = pb("xn", [P, COLS])
        y2 = pb("y2", [P, CHUNK])
        tr = pb("tr", [P, CHUNK])
        tr_b = tr[:, :].bitcast(BF16)

        idx_loaded = sem("idx_loaded")
        sel_loaded = sem("sel_loaded")
        w1_loaded = sem("w1_loaded")
        w2_loaded = sem("w2_loaded")
        deep_loaded = sem("deep_loaded")
        end_loaded = sem("end_loaded")
        w_loaded = [sem(f"w_loaded{i}") for i in range(2)]
        iota_done = sem("iota_done")
        idx_step = sem("idx_step")
        w1_step = sem("w1_step")
        bias_summed = sem("bias_summed")
        idx_staged = sem("idx_staged")
        pool_held = sem("pool_held")
        sp_held = sem("sp_held")
        gathered = sem("gathered")
        split = sem("split")
        lin_done = sem("lin_done")
        x0t_turned = sem("x0t_turned")
        x0t_copied = sem("x0t_copied")
        deep_turned = sem("deep_turned")
        deep_copied = sem("deep_copied")
        spread = sem("spread")
        first_copied = sem("first_copied")
        rows_written = sem("rows_written")
        filled = [sem(f"filled{i}") for i in range(XB_SLOTS)]
        filled_p = [sem(f"filled_p{i}") for i in range(XP_SLOTS)]
        multiplied = sem("multiplied")
        pool_multiplied = sem("pool_multiplied")
        k_made = sem("k_made")
        k_high = sem("k_high")
        k_low = sem("k_low")
        contracted = sem("contracted")
        k_contracted = sem("k_contracted")
        xn_read = sem("xn_read")
        y2_read = sem("y2_read")
        r1_reduced = sem("r1_reduced")
        r1_added = sem("r1_added")
        r2_reduced = sem("r2_reduced")
        r2_added = sem("r2_added")
        acc_ready = sem("acc_ready")
        w_high = sem("w_high")
        w_low = sem("w_low")
        x_high = sem("x_high")
        x_low = sem("x_low")
        h_high = sem("h_high")
        h_low = sem("h_low")
        act_done = sem("act_done")
        out_ready = sem("out_ready")
        row_ready = sem("row_ready")
        stored = sem("stored")

        def spread_by(s, pos, units=UNITS):
            return s * N_SPREADS + (PROLOGUE_UNITS + count(is_spread, units, pos + 1))

        def multiplied_by(s, pos, units=UNITS):
            return s * N_MULTIPLIED + count(is_multiplied, units, pos + 1)

        def contracted_by(s, pos, units=UNITS):
            return s * PAIRS + count(is_l2, units, pos + 1)

        def k_by(s, k):
            return s * K1 + (K1 + k + 1)

        def bc_slot(sl, units, pos):
            return (sl * N_SPREADS + count(is_spread, units, pos)) % 2

        def hp_slot(sl, units, pos):
            return (sl * N_MULTIPLIED + count(is_multiplied, units, pos)) % HP_SLOTS

        def halves_by(s, k):
            return s * K_SPLIT + (K_SPLIT + k + 1)

        def filled_through(per_step, slots, s, sl, slot):
            before = sum(i % slots == slot for i in range(sl * per_step))
            return (s - sl) * (16 * per_step // slots) + 16 * before

        def filled_by(per_step, slots, s, sl, n):
            return (s - sl) * (16 * per_step // slots) + 16 * ((sl * per_step + n) // slots + 1)

        for by, slots in ((BY_DMA, XB_SLOTS), (BY_POOL, XP_SLOTS)):
            assert STEPS * len(by) % slots == 0 and 16 * len(by) % slots == 0

        SPLITS = 4
        GATHERED = 16 * M

        def part(i):
            return parts[:, :, i * M:(i + 1) * M].rearrange("p d m -> p m d")

        def over_tiles(eng, tile):
            tile(0, True, False)
            with eng.Fori(1, TILES - 1) as t:
                tile(t, False, False)
            tile(TILES - 1, False, True)

        N_ACC = len(ACCS)

        def over_groups(eng, group):
            group(0, True, False)
            with eng.Fori(1, GROUPS - 1) as g:
                group(g, False, False)
            group(GROUPS - 1, False, True)

        X_AFTER = {F1N // P + i: range(2 * i, min(2 * i + 2, KD)) for i in range(-(-KD // 2))}

        def x_tile(k):
            return slice(0, LAST_K if k == KD - 1 else P)

        def weights_by(g, a):
            return g * (16 * N_ACC // 2) + 16 * (a // 2 + 1)

        block = ctx.enter_context(nc.Block())

        SEL_LOADED, W1_LOADED, W2_LOADED, DEEP_LOADED, END_LOADED = 64, 48, 48, 80, 112
        ALL_STEPS = TILES * STEPS

        @block.sync
        def _(sp):
            sp.dma_start(raw_idx, sparse.rearrange("(t p) m -> p t m", p=P)).then_inc(idx_loaded, 16)
            for dst, src in ((idb[:, :], ident_b), (selA[:, :], sel_first),
                             (selK[:, :, :], sel_second), (selJ[:, :, :], sel_pair)):
                sp.dma_start(dst, src).then_inc(sel_loaded, 16)
            for dst, src in ((w1a, pair_a), (w1b, pair_b),
                             (bias1[:, :], conv1_b.rearrange("(p o) -> p o", o=1))):
                sp.dma_start(dst, src).then_inc(w1_loaded, 16)
            sp.dma_start(w2s[:, :, :], w2rows).then_inc(w2_loaded, 16)
            for c in range(2):
                sp.dma_start(bias2[H * c:H * c + H, :], conv2_b[H:2 * H].rearrange("(p o) -> p o", o=1)).then_inc(w2_loaded, 16)
            for dst, src in ((idf[:, :], ident_f),
                             (deep_t[LAST_E:LAST_K, KD - 1, :], dense_t),
                             (bd1[:, :], b1), (bd2[:, :], b2), (bd3[:, :], b3)):
                sp.dma_start(dst, src).then_inc(deep_loaded, 16)
            for dst, src in ((wdo[:, :], deep_w),
                             (cw1[0:H, :], cin_w[0:H, :]), (cw1[H:P, :], cin_w[0:H, :]),
                             (cw2[0:H, :], cin_w[H:2 * H, :]),
                             (cw2[H:P, :], cin_w[H:2 * H, :]),
                             (cwd[:, :], lin_dense.rearrange("(p o) -> p o", o=1)),
                             (sc3[:, :], scalars)):
                sp.dma_start(dst, src).then_inc(end_loaded, 16)

            def load_weights(a):
                layer, m = ACCS[a]
                sp.dma_start(w_raw[a % 2][:, 0:LAYER_ROWS[layer], :], (W1, W2, W3)[layer][m]).then_inc(w_loaded[a % 2], 16)

            load_weights(0)

            def hold():
                sp.sem_inc(sp_held, 1)

            def write_rows(s, sl):
                sp.wait_ge(first_copied, s + 1)
                hold()
                sp.dma_start(rows[sl % 2, :, :], first[sl % 2][0:M, :]).then_inc(rows_written, 16)

            def spread_rows(sl, unit):
                return rows[sl % 2, 2 * unit:2 * unit + 2, :].unsqueeze(1).to_broadcast([2, H, COLS])

            def fill(s, sl, by, n, is_first):
                if by == BY_DMA:
                    slot = (sl * len(BY_DMA) + n) % XB_SLOTS
                    if n >= XB_SLOTS:
                        units = UNITS_LAST if is_final(s) else UNITS
                        sp.wait_ge(multiplied, multiplied_by(s, units.index(BY_DMA[n - XB_SLOTS]), units))
                        hold()
                    elif not is_first:
                        sp.wait_ge(multiplied, multiplied_by(s - 1, UNITS.index(BY_DMA[n - XB_SLOTS])))
                        hold()
                    sp.dma_start(xb[slot][:, :], spread_rows(sl, BY_DMA[n])).then_inc(filled[slot], 16)
                else:
                    slot = (sl * len(BY_POOL) + n) % XP_SLOTS
                    if not is_first:
                        sp.wait_ge(pool_multiplied, s * len(BY_POOL) + (n - XP_SLOTS + 1))
                        hold()
                    sp.dma_start(xp[slot][:, :], spread_rows(sl, BY_POOL[n])).then_inc(filled_p[slot], 16)

            fills = []
            for by, slots in ((BY_DMA, XB_SLOTS), (BY_POOL, XP_SLOTS)):
                for n in range(len(by)):
                    fills.append((UNITS.index(by[n - slots]), int(n < slots), by, n))
            fills.sort()

            def is_final(s):
                return isinstance(s, int) and s == ALL_STEPS - 1

            write_rows(0, 0)
            sp.wait_ge(rows_written, 16)
            for _, ahead, by, n in fills:
                if ahead:
                    fill(0, 0, by, n, True)

            def tile(t, is_first, is_last):
                for sl in range(STEPS):
                    s = t * STEPS + sl
                    final = is_last and sl == STEPS - 1
                    if not final:
                        if not (is_first and sl == 0):
                            for i in range(XB_SLOTS):
                                sp.wait_ge(filled[i], filled_through(len(BY_DMA), XB_SLOTS, s, sl, i))
                                hold()
                            for i in range(XP_SLOTS):
                                sp.wait_ge(filled_p[i], filled_through(len(BY_POOL), XP_SLOTS, s, sl, i))
                                hold()
                        write_rows(s + 1, sl + 1)
                    written = False
                    for _, ahead, by, n in fills:
                        if ahead and not written and not final:
                            sp.wait_ge(rows_written, s * 16 + 32)
                            hold()
                            written = True
                        if not ahead:
                            fill(s, sl, by, n, False)
                        elif not final:
                            fill(s + 1, sl + 1, by, n, False)

            over_tiles(sp, tile)

            sp.wait_ge(contracted, ALL_STEPS * PAIRS)
            load_weights(1)

            def deep_group(g, is_first, is_last):
                for a in range(N_ACC):
                    if not (is_last and a + 2 >= N_ACC):
                        sp.wait_ge(w_low, g * N_ACC + (a + 1))
                        hold()
                        load_weights((a + 2) % N_ACC)

            over_groups(sp, deep_group)
            sp.wait_ge(row_ready, GROUPS)
            sp.dma_start(out.rearrange("(g n) -> g n", n=CHUNK),
                         orow[0:32 * (GROUPS - 1) + 1:32, :]).then_inc(stored, 16)
            sp.wait_ge(stored, 16)

        @block.gpsimd
        def _(pool):
            nc.gpsimd.iota(field_base, [[0, TILES], [V, M]], base=0, channel_multiplier=0).then_inc(iota_done, 1)

            def hold():
                pool.sem_inc(pool_held, 1)

            def stage(t):
                hold()
                nc.gpsimd.tensor_copy(idx_stage[:, :], idx_all[:, bass.ds(t, 1), :].rearrange("p a m -> p (a m)")).then_inc(idx_staged, 1)
                pool.wait_ge(idx_staged, t + 1)
                hold()

            def gather(fields):
                for m in fields:
                    nc.gpsimd.indirect_dma_start(
                        out=emb[:, m, :], out_offset=None, in_=table,
                        in_offset=bass.IndirectOffsetOnAxis(ap=idx_stage[:, m:m + 1], axis=0)).then_inc(gathered, 16)

            def split_parts(t):
                pool.wait_ge(split, t * SPLITS + 1)
                nc.gpsimd.tensor_tensor(rem[:, :, :], emb[:, :, 0:D], part(0), ALU.subtract).then_inc(split, 1)
                pool.wait_ge(split, t * SPLITS + 3)
                nc.gpsimd.tensor_tensor(part(2), rem[:, :, :], part(1), ALU.subtract).then_inc(split, 1)

            def multiply(t, sl, n, is_start):
                s = t * STEPS + sl
                slot = (sl * len(BY_POOL) + n) % XP_SLOTS
                if n == 0:
                    pool.wait_ge(xn_read, s + 1)
                pool.wait_ge(filled_p[slot], filled_by(len(BY_POOL), XP_SLOTS, s, sl, n))
                if not is_start:
                    pool.wait_ge(contracted, contracted_by(s - 1, UNITS.index(BY_POOL[n])))
                nc.gpsimd.tensor_tensor(pp[n][:, :], xp[slot][:, :], xk[sl % 2][:, :], ALU.mult).then_inc(pool_multiplied, 1)

            pool.wait_ge(idx_step, 4)
            stage(0)
            gather(range(M))

            def tile(t, is_first, is_last):
                early = len(BY_POOL) if is_first else 0
                run = -(-M // (2 * len(BY_POOL) - early))
                for n in range(2 * len(BY_POOL)):
                    if n == early and not is_last:
                        pool.wait_ge(split, t * SPLITS + SPLITS)
                        pool.wait_ge(deep_turned, t * 2 + 2)
                        pool.wait_ge(lin_done, t + 1)
                        stage(t + 1)
                    if n >= early and not is_last:
                        gather(range((n - early) * run, min(M, (n - early + 1) * run)))
                    multiply(t, n // len(BY_POOL), n % len(BY_POOL), is_first and n < len(BY_POOL))
                if not is_last:
                    split_parts(t + 1)
                for sl in (2, 3):
                    for n in range(len(BY_POOL)):
                        multiply(t, sl, n, False)

            over_tiles(pool, tile)

        @block.vector
        def _(dve):
            dve.wait_ge(idx_loaded, 16)
            nc.vector.tensor_scalar(wrapped, raw_idx, 0.0, float(V), ALU.is_lt, ALU.mult).then_inc(idx_step, 1)
            dve.wait_ge(idx_step, 1)
            nc.vector.tensor_tensor(wrapped, wrapped, raw_idx, ALU.add).then_inc(idx_step, 1)
            dve.wait_ge(idx_step, 2)
            nc.vector.tensor_scalar(wrapped, wrapped, 0.0, float(V - 1), ALU.max, ALU.min).then_inc(idx_step, 1)
            dve.wait_ge(idx_step, 3)
            dve.wait_ge(iota_done, 1)
            nc.vector.tensor_tensor(idx_all[:, :, :], wrapped, field_base, ALU.add).then_inc(idx_step, 1)
            dve.wait_ge(w1_loaded, W1_LOADED)
            nc.vector.tensor_tensor(w1s[:, :, :], w1a, w1b, ALU.add).then_inc(w1_step, 1)
            dve.wait_ge(w1_step, 1)
            nc.vector.tensor_copy(w1_hi[:, :, :], w1s[:, 0:K_SPLIT, :]).then_inc(w1_step, 1)
            dve.wait_ge(w1_step, 2)
            nc.vector.tensor_tensor(w1_lo[:, :, :], w1s[:, 0:K_SPLIT, :], w1_hi[:, :, :], ALU.subtract).then_inc(w1_step, 1)
            dve.wait_ge(end_loaded, END_LOADED)
            nc.vector.tensor_reduce(bias_out[:, :], sc3[:, :], AX_X, ALU.add).then_inc(bias_summed, 1)
            dve.wait_ge(gathered, GATHERED)
            nc.vector.tensor_copy(part(0), emb[:, :, 0:D]).then_inc(split, 1)
            dve.wait_ge(split, 1)
            nc.vector.tensor_tensor(rem[:, :, :], emb[:, :, 0:D], part(0), ALU.subtract).then_inc(split, 1)
            dve.wait_ge(split, 2)
            nc.vector.tensor_copy(part(1), rem[:, :, :]).then_inc(split, 1)
            dve.wait_ge(split, 3)
            nc.vector.tensor_tensor(part(2), rem[:, :, :], part(1), ALU.subtract).then_inc(split, 1)

            def sum_linear(t):
                dve.wait_ge(gathered, t * GATHERED + GATHERED)
                nc.vector.tensor_reduce(lin_sum[:, bass.ds(t, 1)], emb[:, :, D], AX_X, ALU.add).then_inc(lin_done, 1)

            sum_linear(0)

            def k_product(s, sl, k, spread_count, slot, is_early):
                if k == 0:
                    dve.wait_ge(first_copied, s + 2)
                dve.wait_ge(spread, spread_count)
                if k >= K_SPLIT and not is_early:
                    dve.wait_ge(k_contracted, k_by(s, k) - K1)
                nc.vector.tensor_tensor(kp[k][:, :], bc[slot][:, :], first[(sl + 1) % 2][:, :], ALU.mult).then_inc(k_made, 1)

            def k_lower(s, k, is_early):
                dve.wait_ge(k_high, halves_by(s, k))
                if not is_early:
                    dve.wait_ge(k_contracted, k_by(s, k) - K1)
                nc.vector.tensor_tensor(k_lo[k][:, :], kp[k][:, :], k_hi[k][:, :], ALU.subtract).then_inc(k_low, 1)

            for k in range(K1):
                k_product(-1, -1, k, 2 + k, (1 + k) % 2, True)
                if k < K_SPLIT:
                    k_lower(-1, k, True)

            def reduce_r1(t, sl):
                s = t * STEPS + sl
                dve.wait_ge(xn_read, s + 1)
                if sl > 0:
                    if sl > 1 or not isinstance(t, int) or t > 0:
                        dve.wait_ge(r1_added, t * (STEPS - 1) + (sl - 1))
                    dst = tmp1[:, :]
                else:
                    dst = sum1[:, bass.ds(t * P, P)]
                nc.vector.tensor_reduce(dst, r1[sl % 2][:, :].rearrange("p (q b) -> p b q", b=P), AX_X, ALU.add).then_inc(r1_reduced, 1)

            def add_r1(t, sl):
                dve.wait_ge(r1_reduced, t * STEPS + (sl + 1))
                acc = sum1[:, bass.ds(t * P, P)]
                nc.vector.tensor_tensor(acc, acc, tmp1[:, :], ALU.add).then_inc(r1_added, 1)

            def reduce_r2(t, sl):
                s = t * STEPS + sl
                dve.wait_ge(y2_read, s + 1)
                if sl > 0:
                    if sl > 1 or not isinstance(t, int) or t > 0:
                        dve.wait_ge(r2_added, t * (STEPS - 1) + (sl - 1))
                    dst = tmp2[:, :]
                else:
                    dst = sum2[:, bass.ds(t * P, P)]
                nc.vector.tensor_reduce(dst, r2[sl % 2][:, :].rearrange("p (q b) -> p b q", b=P), AX_X, ALU.add).then_inc(r2_reduced, 1)

            def add_r2(t, sl):
                dve.wait_ge(r2_reduced, t * STEPS + (sl + 1))
                acc = sum2[:, bass.ds(t * P, P)]
                nc.vector.tensor_tensor(acc, acc, tmp2[:, :], ALU.add).then_inc(r2_added, 1)

            def tile(t, is_first, is_last):
                for sl in range(STEPS):
                    s = t * STEPS + sl
                    start = is_first and sl == 0
                    units = UNITS_LAST if is_last and sl == STEPS - 1 else UNITS
                    before = (t, sl - 1) if sl else (t - 1, STEPS - 1)
                    split_k = None
                    for pos, unit in enumerate(units):
                        if is_k(unit):
                            if split_k is not None:
                                k_lower(s, split_k, False)
                                split_k = None
                            slot = bc_slot(sl, units, pos)
                            k_product(s, sl, unit[1], spread_by(s, pos), slot, False)
                            if unit[1] < K_SPLIT:
                                split_k = unit[1]
                        elif is_multiplied(unit):
                            if unit == 0:
                                dve.wait_ge(xn_read, s + 1)
                            if is_spread(unit):
                                dve.wait_ge(spread, spread_by(s, pos, units))
                                x = bc[bc_slot(sl, units, pos)]
                            else:
                                n = BY_DMA.index(unit)
                                xb_slot = (sl * len(BY_DMA) + n) % XB_SLOTS
                                x = xb[xb_slot]
                                dve.wait_ge(filled[xb_slot], filled_by(len(BY_DMA), XB_SLOTS, s, sl, n))
                            mine = [u for u in units if is_multiplied(u)]
                            at = mine.index(unit)
                            if at >= HP_SLOTS:
                                dve.wait_ge(contracted, contracted_by(s, units.index(mine[at - HP_SLOTS]), units))
                            elif not start:
                                dve.wait_ge(contracted, contracted_by(s - 1, UNITS.index(mine[at - HP_SLOTS])))
                            nc.vector.tensor_tensor(hp[hp_slot(sl, units, pos)][:, :], x[:, :], xk[sl % 2][:, :], ALU.mult).then_inc(multiplied, 1)
                            if split_k is not None:
                                k_lower(s, split_k, False)
                                split_k = None
                        if unit == 1:
                            reduce_r1(t, sl)
                        if unit == 4 and sl:
                            add_r1(t, sl)
                        if unit == 6 and not start:
                            reduce_r2(*before)
                        if unit == 8 and not start and before[1]:
                            add_r2(*before)
                        if unit == 5 and sl == STEPS - 1 and not is_last:
                            sum_linear(t + 1)

            over_tiles(dve, tile)
            def lower_x(g, k):
                dve.wait_ge(x_high, g * KD + (k + 1))
                rows = x_tile(k)
                nc.vector.tensor_tensor(x_lo[rows, k, :], deep_t[rows, k, bass.ds(g * CHUNK, CHUNK)], x_hi[rows, k, :],
                                        ALU.subtract).then_inc(x_low, 1)

            def lower_w(g, a):
                dve.wait_ge(w_high, g * N_ACC + (a + 1))
                ks = slice(0, LAYER_ROWS[ACCS[a % N_ACC][0]])
                nc.vector.tensor_tensor(w_lo[a % 2][:, ks, :], w_raw[a % 2][:, ks, :], w_hi[a % 2][:, ks, :],
                                        ALU.subtract).then_inc(w_low, 1)

            for k in range(KD):
                lower_x(0, k)
            lower_w(0, 0)
            reduce_r2(TILES - 1, STEPS - 1)
            add_r2(TILES - 1, STEPS - 1)

            def deep_group(g, is_first, is_last):
                for a in range(N_ACC):
                    if not (is_last and a == N_ACC - 1):
                        lower_w(g, a + 1)
                    if a < HIDDEN:
                        dve.wait_ge(h_high, g * HIDDEN + (a + 1))
                        nc.vector.tensor_tensor(h_lo[:, a, :], h_raw[a % 2][:, :], h_hi[:, a, :], ALU.subtract).then_inc(h_low, 1)
                    if a in X_AFTER and not is_last:
                        for k in X_AFTER[a]:
                            lower_x(g + 1, k)

            over_groups(dve, deep_group)

        @block.tensor
        def _(pe):
            def turn_x0(sl):
                for q in range(STEP_D):
                    last = nc.tensor.transpose(tr_b[0:PM, q * P:(q + 1) * P], parts[:, sl * STEP_D + q, :], idb[:, :])
                last.then_inc(x0t_turned, 1)

            def turn_deep(half):
                numbers = emb[:, :, :].rearrange("p m e -> p (m e)")
                for i, k in enumerate((range(4), range(4, KD))[half]):
                    n = min(P, M * ROW - k * P)
                    last = nc.tensor.transpose(tr[0:n, i * P:(i + 1) * P], numbers[:, k * P:k * P + n], idf[:, :])
                last.then_inc(deep_turned, 1)

            def broadcast(unit, slot, sl):
                x = x0t[sl % 2] if is_l2(unit) else x0t[(sl + 1) % 2]
                sel = selJ[:, unit, :] if is_l2(unit) else selA[:, :] if unit == "A" else selK[:, unit[1], :]
                for c in range(2):
                    last = nc.tensor.matmul(bc[slot][:, c * CHUNK:(c + 1) * CHUNK], sel, x[:, c * CHUNK:(c + 1) * CHUNK],
                                            start=True, stop=True)
                last.then_inc(spread, 1)

            def bc_left(s, k):
                pe.wait_ge(k_made, k_by(s, k))

            def contract_k(s, sl, k, is_first):
                if k == 0 and not is_first:
                    pe.wait_ge(xn_read, s + 1)
                if k < K_SPLIT:
                    pe.wait_ge(k_high, halves_by(s, k))
                    pe.wait_ge(k_low, halves_by(s, k))
                    passes = ((w1_hi, k_hi[k]), (w1_lo, k_hi[k]), (w1_hi, k_lo[k]))
                else:
                    pe.wait_ge(k_made, k_by(s, k))
                    passes = ((w1s, kp[k]),)
                for i, (w, x) in enumerate(passes):
                    for c in range(2):
                        cols = slice(c * CHUNK, (c + 1) * CHUNK)
                        last = nc.tensor.matmul(xn[:, cols], w[:, k, :], x[:, cols],
                                                start=(k == 0 and i == 0), stop=(k == K1 - 1))
                last.then_inc(k_contracted, 1)

            def contract(s, sl, pos, units, is_start):
                unit = units[pos]
                if unit == 0 and not is_start:
                    pe.wait_ge(y2_read, s)
                if unit in BY_POOL:
                    n = BY_POOL.index(unit)
                    pe.wait_ge(pool_multiplied, s * len(BY_POOL) + (n + 1))
                    src = pp[n]
                else:
                    pe.wait_ge(multiplied, multiplied_by(s, pos, units))
                    src = hp[hp_slot(sl, units, pos)]
                for c in range(2):
                    last = nc.tensor.matmul(y2[H * c:H * c + H, :], w2s[:, unit, :], src[:, c * CHUNK:(c + 1) * CHUNK],
                                            start=(unit == 0), stop=(unit == PAIRS - 1))
                last.then_inc(contracted, 1)

            pe.wait_ge(sel_loaded, SEL_LOADED)
            pe.wait_ge(split, SPLITS)
            turn_x0(0)
            pe.wait_ge(x0t_copied, 1)
            broadcast("A", 0, -1)
            broadcast(("K", 0), 1, -1)
            turn_x0(1)
            pe.wait_ge(first_copied, 1)
            broadcast(("K", 1), 0, -1)
            bc_left(-1, 0)
            broadcast(("K", 2), 1, -1)
            pe.wait_ge(w1_step, 3)
            for k in range(K1):
                contract_k(-1, -1, k, True)
            pe.wait_ge(deep_loaded, DEEP_LOADED)
            pe.wait_ge(w2_loaded, W2_LOADED)

            def tile(t, is_first, is_last):
                for sl in range(STEPS):
                    s = t * STEPS + sl
                    start = is_first and sl == 0
                    final = is_last and sl == STEPS - 1
                    units = UNITS_LAST if final else UNITS
                    for pos, unit in enumerate(units):
                        if pos == 0:
                            pe.wait_ge(x0t_copied, s + (1 if final else 2))
                        if is_spread(unit):
                            mine = [q for q in range(len(units)) if is_spread(units[q])]
                            at = mine.index(pos)
                            q = mine[at - 2] if at >= 2 else [q for q in range(len(UNITS)) if is_spread(UNITS[q])][at - 2]
                            of, us, ss = (UNITS[q], UNITS, s - 1) if at < 2 else (units[q], units, s)
                            if at < 2 and start:
                                bc_left(-1, K1 - 2 + at)
                            elif of == "A":
                                pe.wait_ge(first_copied, ss + 2)
                            elif is_k(of):
                                bc_left(ss, of[1])
                            else:
                                pe.wait_ge(multiplied, multiplied_by(ss, q, us))
                            broadcast(unit, bc_slot(sl, units, pos), sl)
                        if pos in POS_DEEP and (start or (sl == STEPS - 1 and not is_last)):
                            half = POS_DEEP.index(pos)
                            if half:
                                pe.wait_ge(deep_copied, 1 if start else t * 2 + 3)
                            turn_deep(half)
                        if pos == POS_TURN and not (is_last and sl >= 2):
                            if sl == STEPS - 1 or (is_first and sl == 0):
                                pe.wait_ge(deep_copied, t * 2 + (4 if sl else 2))
                            if sl == 2:
                                pe.wait_ge(split, t * SPLITS + 2 * SPLITS)
                            turn_x0((sl + 2) % STEPS)
                        if pos >= K_LAG and is_k(units[pos - K_LAG]):
                            contract_k(s, sl, units[pos - K_LAG][1], False)
                        if pos >= L2_LAG and is_l2(units[pos - L2_LAG]):
                            contract(s, sl, pos - L2_LAG, units, start)
                        elif pos < L2_LAG and not start:
                            contract(s - 1, sl - 1, len(UNITS) - L2_LAG + pos, UNITS, False)
                if is_last:
                    for pos in range(PAIRS - L2_LAG, PAIRS):
                        contract(ALL_STEPS - 1, STEPS - 1, pos, UNITS_LAST, False)

            over_tiles(pe, tile)

            def deep_group(g, is_first, is_last):
                for a, (layer, m) in enumerate(ACCS):
                    pe.wait_ge(w_high, g * N_ACC + (a + 1))
                    pe.wait_ge(w_low, g * N_ACC + (a + 1))
                    if not (is_first and a < 2):
                        pe.wait_ge(act_done, g * N_ACC + (a - 1))
                    rows = LAYER_ROWS[layer]
                    for k in range(rows):
                        part = x_tile(k) if layer == 0 else slice(0, P)
                        if layer == 0:
                            hi, lo, at = x_hi, x_lo, k
                            if m == 0:
                                pe.wait_ge(x_high, g * KD + (k + 1))
                                pe.wait_ge(x_low, g * KD + (k + 1))
                        else:
                            hi, lo, at = h_hi, h_lo, (layer - 1) * (F1N // P) + k
                            if m == 0:
                                pe.wait_ge(h_high, g * HIDDEN + (at + 1))
                                pe.wait_ge(h_low, g * HIDDEN + (at + 1))
                        for i, (w, x) in enumerate(((w_hi, hi), (w_lo, hi), (w_hi, lo))):
                            last = nc.tensor.matmul(bc[a % 2][:, 0:CHUNK], w[a % 2][part, k, :], x[part, at, :],
                                                    start=(k == 0 and i == 0), stop=(k == rows - 1 and i == 2))
                    last.then_inc(acc_ready, 1)

            pe.wait_ge(multiplied, ALL_STEPS * N_MULTIPLIED)
            over_groups(pe, deep_group)

            pe.wait_ge(end_loaded, END_LOADED)
            pe.wait_ge(xn_read, ALL_STEPS)
            pe.wait_ge(r1_reduced, ALL_STEPS)
            pe.wait_ge(r1_added, TILES * (STEPS - 1))
            pe.wait_ge(r2_added, TILES * (STEPS - 1))
            pe.wait_ge(lin_done, TILES)
            terms = [(cw1[:, :], sum1[:, :]), (cw2[:, :], sum2[:, :]), (cwd[:, :], deep_t[0:LAST_K, KD - 1, :])]
            terms += [(wdo[:, k:k + 1], h3[:, k, :]) for k in range(F3N // P)]
            for n, (w, x) in enumerate(terms):
                if n == 3:
                    pe.wait_ge(act_done, GROUPS * N_ACC)
                for g in range(GROUPS):
                    nc.tensor.matmul(xn[32 * g:32 * g + 1, 0:CHUNK], w, x[:, g * CHUNK:(g + 1) * CHUNK],
                                     start=(n == 0), stop=False, skip_group_check=True)
            for c in range(CHUNK // P):
                for g in range(GROUPS):
                    t = g * (CHUNK // P) + c
                    last = nc.tensor.matmul(xn[32 * g:32 * g + 1, c * P:(c + 1) * P], lin_sum[:, t:t + 1], idf[:, :],
                                            start=False, stop=True, skip_group_check=True)
            last.then_inc(out_ready, 1)

        @block.scalar
        def _(act):
            act.wait_ge(w1_loaded, W1_LOADED)
            nc.scalar.activation(xk[0][:, 0:1], bias1[:, :], ACT.Sigmoid)

            def copy_x0(s, sl):
                act.wait_ge(x0t_turned, s + 1)
                nc.scalar.activation(x0t[sl % 2][:, :], tr_b[0:PM, :], ACT.Copy).then_inc(x0t_copied, 1)

            def copy_deep(t, half):
                act.wait_ge(deep_turned, t * 2 + (half + 1))
                cols = bass.ds(t * P, P)
                if half == 0:
                    nc.scalar.activation(deep_t[:, 0:4, cols], tr[:, :].rearrange("p (k b) -> p k b", b=P),
                                         ACT.Copy).then_inc(deep_copied, 1)
                else:
                    nc.scalar.activation(deep_t[:, 4:6, cols], tr[:, 0:2 * P].rearrange("p (k b) -> p k b", b=P), ACT.Copy)
                    nc.scalar.activation(deep_t[0:LAST_E, 6, cols], tr[0:LAST_E, 2 * P:3 * P],
                                         ACT.Copy).then_inc(deep_copied, 1)

            def upper(s, k, is_early):
                act.wait_ge(k_made, k_by(s, k))
                if not is_early:
                    act.wait_ge(k_contracted, k_by(s, k) - K1)
                nc.scalar.activation(k_hi[k][:, :], kp[k][:, :], ACT.Copy).then_inc(k_high, 1)

            def read_xn(slot):
                nc.scalar.activation(xk[slot][0:H, :], xn[0:H, :], ACT.Sigmoid, bias=bias1[0:H, :])
                nc.scalar.activation(xk[slot][H:P, :], xn[0:H, :], ACT.Sigmoid, bias=bias1[0:H, :])
                for c in range(2):
                    last = nc.scalar.activation(r1[slot][H * c:H * c + H, :], xn[H:P, c * CHUNK:(c + 1) * CHUNK],
                                                ACT.Sigmoid, bias=bias1[H:P, :])
                last.then_inc(xn_read, 1)

            def read_y2(s, slot, is_early):
                act.wait_ge(contracted, s * PAIRS + PAIRS)
                if not is_early:
                    act.wait_ge(r2_reduced, s - 1)
                nc.scalar.activation(r2[slot][:, :], y2[:, :], ACT.Sigmoid, bias=bias2[:, :]).then_inc(y2_read, 1)

            copy_x0(0, 0)
            act.wait_ge(spread, 1)
            nc.scalar.activation(first[0][:, :], bc[0][:, :], ACT.Copy).then_inc(first_copied, 1)
            copy_x0(1, 1)
            for k in range(K_SPLIT):
                upper(-1, k, True)
            act.wait_ge(k_contracted, K1)
            read_xn(0)
            act.wait_ge(w2_loaded, W2_LOADED)

            def tile(t, is_first, is_last):
                for sl in range(STEPS):
                    s = t * STEPS + sl
                    start = is_first and sl == 0
                    final = is_last and sl == STEPS - 1
                    units = UNITS_LAST if final else UNITS
                    for pos, unit in enumerate(units):
                        if unit == "A":
                            act.wait_ge(spread, spread_by(s, pos))
                            if not start:
                                act.wait_ge(k_made, s * K1)
                                act.wait_ge(rows_written, s * 16)
                            nc.scalar.activation(first[(sl + 1) % 2][:, :], bc[bc_slot(sl, UNITS, pos)][:, :],
                                                 ACT.Copy).then_inc(first_copied, 1)
                        if pos == L2_LAG and not start:
                            read_y2(s - 1, (sl + 1) % 2, is_first and sl <= 2)
                        if pos - 1 in POS_DEEP and (start or (sl == STEPS - 1 and not is_last)):
                            copy_deep(0 if start else t + 1, POS_DEEP.index(pos - 1))
                        if is_k(unit) and unit[1] < K_SPLIT:
                            upper(s, unit[1], False)
                    if final:
                        continue
                    if sl == 2 and not is_last:
                        act.wait_ge(gathered, t * GATHERED + 2 * GATHERED)
                        act.wait_ge(x0t_turned, t * STEPS + STEPS)
                        nc.scalar.activation(part(0), emb[:, :, 0:D], ACT.Copy).then_inc(split, 1)
                        act.wait_ge(split, t * SPLITS + (SPLITS + 2))
                        nc.scalar.activation(part(1), rem[:, :, :], ACT.Copy).then_inc(split, 1)
                    if not (is_last and sl >= 2):
                        act.wait_ge(spread, s * N_SPREADS + (PROLOGUE_UNITS + N_SPREADS))
                        copy_x0(s + 2, sl + 2)
                    act.wait_ge(k_contracted, k_by(s, K1 - 1))
                    if not start:
                        act.wait_ge(multiplied, s * N_MULTIPLIED)
                        act.wait_ge(pool_multiplied, s * len(BY_POOL))
                        act.wait_ge(r1_reduced, s)
                    read_xn((sl + 1) % 2)

            over_tiles(act, tile)
            def upper_x(g, k):
                rows = x_tile(k)
                nc.scalar.activation(x_hi[rows, k, :], deep_t[rows, k, bass.ds(g * CHUNK, CHUNK)],
                                     ACT.Copy).then_inc(x_high, 1)

            def upper_w(g, a):
                act.wait_ge(w_loaded[a % 2], weights_by(g, a))
                ks = slice(0, LAYER_ROWS[ACCS[a % N_ACC][0]])
                nc.scalar.activation(w_hi[a % 2][:, ks, :], w_raw[a % 2][:, ks, :], ACT.Copy).then_inc(w_high, 1)

            act.wait_ge(deep_loaded, DEEP_LOADED)
            act.wait_ge(k_contracted, ALL_STEPS * K1)
            act.wait_ge(rows_written, ALL_STEPS * 16)
            for k in range(KD):
                upper_x(0, k)
            read_y2(ALL_STEPS - 1, (ALL_STEPS - 1) % 2, False)
            upper_w(0, 0)

            def deep_group(g, is_first, is_last):
                for a, (layer, m) in enumerate(ACCS):
                    base = g * N_ACC
                    if not (is_last and a == N_ACC - 1):
                        if not (is_first and a == 0):
                            act.wait_ge(acc_ready, base + a)
                        upper_w(g, a + 1)
                    act.wait_ge(acc_ready, base + (a + 1))
                    bias = (bd1, bd2, bd3)[layer][:, m:m + 1]
                    if a >= HIDDEN:
                        nc.scalar.activation(h3[:, m, bass.ds(g * CHUNK, CHUNK)], bc[a % 2][:, 0:CHUNK], ACT.Tanh,
                                             bias=bias).then_inc(act_done, 1)
                    else:
                        if not (is_first and a < 2):
                            act.wait_ge(h_low, g * HIDDEN + (a - 1))
                        nc.scalar.activation(h_raw[a % 2][:, :], bc[a % 2][:, 0:CHUNK], ACT.Tanh, bias=bias).then_inc(act_done, 1)
                        act.wait_ge(act_done, base + (a + 1))
                        nc.scalar.activation(h_hi[:, a, :], h_raw[a % 2][:, :], ACT.Copy).then_inc(h_high, 1)
                    if a in X_AFTER and not is_last:
                        for k in X_AFTER[a]:
                            upper_x(g + 1, k)

            over_groups(act, deep_group)
            act.wait_ge(bias_summed, 1)
            act.wait_ge(out_ready, 1)
            for g in range(GROUPS):
                r = slice(32 * g, 32 * g + 1)
                nc.scalar.activation(orow[r, :], xn[r, 0:CHUNK], ACT.Identity, bias=bias_out[r, :]).then_inc(row_ready, 1)


def kernel(r_dense, r_sparse, L0_rec_tables, L0_rec_lin_sparse_w, L0_rec_lin_dense_w, L0_rec_conv1_w,
           L0_rec_conv1_b, L0_rec_conv2_w, L0_rec_conv2_b, L0_rec_cin_w, L0_rec_cin_b, L0_rec_W1, L0_rec_b1,
           L0_rec_W2, L0_rec_b2, L0_rec_W3, L0_rec_b3, L0_rec_deep_w, L0_rec_deep_b, L0_rec_bias):
    import concourse.bacc as _bacc
    from concourse import mybir as _mybir
    from concourse.bass_utils import run_bass_kernel_spmd as _run

    f = np.asarray
    table = np.concatenate([f(L0_rec_tables).reshape(M * V, D), f(L0_rec_lin_sparse_w).reshape(M * V, 1)], axis=1)
    w1t = np.concatenate([f(L0_rec_conv1_w).T, np.zeros((1, P), np.float32)])
    row_a = np.full((P, K1), M * M)
    row_b = np.full((P, K1), M * M)
    second = pair_rows()
    for (k, p), m in second.items():
        h = p % M
        row_a[p, k] = h * M + m
        if m != h:
            row_b[p, k] = m * M + h
    w2 = f(L0_rec_conv2_w)[H:].reshape(H, H, PAIRS, 2).transpose(3, 1, 2, 0).reshape(P, PAIRS, H)
    deep1 = np.zeros((KD * P, F1N), np.float32)
    deep1[:M * ROW].reshape(M, ROW, F1N)[:, :D] = f(L0_rec_W1)[:M * D].reshape(M, D, F1N)
    deep1[M * ROW:DEEP_ROWS] = f(L0_rec_W1)[M * D:]
    def by_tile(w):
        return w.reshape(-1, P, w.shape[1] // P, P).transpose(2, 1, 0, 3)

    bf = _mybir.dt.np(_mybir.dt.bfloat16)
    sel_first = np.zeros((PARTS, M, P), bf)
    sel_second = np.zeros((PARTS, M, K1, P), bf)
    sel_pair = np.zeros((PARTS, M, PAIRS, P), bf)
    for p in range(P):
        sel_first[:, p % M, p] = 1
        for j in range(PAIRS):
            sel_pair[:, 2 * j + p // H, j, p] = 1
    for (k, p), m in second.items():
        sel_second[:, m, k, p] = 1

    ins = {
        "table": table, "sparse": f(r_sparse), "dense_t": f(r_dense).T, "lin_dense": np.concatenate([np.zeros(LAST_E, np.float32), f(L0_rec_lin_dense_w)]),
        "pair_a": w1t[row_a], "pair_b": w1t[row_b], "w2rows": w2, "conv1_b": f(L0_rec_conv1_b),
        "conv2_b": f(L0_rec_conv2_b), "cin_w": f(L0_rec_cin_w),
        "scalars": np.tile(np.concatenate([f(L0_rec_cin_b), f(L0_rec_deep_b), f(L0_rec_bias)]), (P, 1)),
        "W1": by_tile(deep1), "b1": f(L0_rec_b1).reshape(-1, P).T, "W2": by_tile(f(L0_rec_W2)), "b2": f(L0_rec_b2).reshape(-1, P).T, "W3": by_tile(f(L0_rec_W3)),
        "b3": f(L0_rec_b3).reshape(-1, P).T, "deep_w": f(L0_rec_deep_w).reshape(-1, P).T,
        "sel_first": sel_first.reshape(PM, P), "sel_second": sel_second.reshape(PM, K1, P),
        "sel_pair": sel_pair.reshape(PM, PAIRS, P),
        "ident_b": np.eye(P, dtype=bf), "ident_f": np.eye(P, dtype=np.float32),
    }
    nc = _bacc.Bacc("TRN2", target_bir_lowering=False, num_devices=1)
    arrays, args = {}, []
    for name, a in ins.items():
        a = np.ascontiguousarray(a)
        arrays[name] = a
        args.append(nc.dram_tensor(name, a.shape, _mybir.dt.from_np(a.dtype), kind="ExternalInput").ap())
    args.append(nc.dram_tensor("result", (B,), _mybir.dt.float32, kind="ExternalOutput").ap())
    build(nc, *args)
    r = _run(nc, [arrays], core_ids=[0])
    return r.results[0]["result"]
```
